# Optimizing a Trainium2 kernel written in Bass

```python
import numpy as np
import jax
import jax.numpy as jnp

def _softmax(x, axis=-1):
    return jax.nn.softmax(x, axis=axis)

def _gelu(x):
    return jax.nn.gelu(x, approximate=True)

def _silu(x):
    return jax.nn.silu(x)

def _sigmoid(x):
    return jax.nn.sigmoid(x)

def _layernorm(x, axis=-1, eps=1e-05):
    m = jnp.mean(x, axis=axis, keepdims=True)
    v = jnp.var(x, axis=axis, keepdims=True)
    return (x - m) / jnp.sqrt(v + eps)

def _scatter_add(tgt, idx, src, axis=0):
    return tgt.at[idx].add(src)

def _segment_sum(src, seg, n):
    return jax.ops.segment_sum(src, seg, n)
kernel_name = 'mk_adaln_d1_jaxref_r8_e93e4c'

def setup_inputs(seed: int=0):
    np.random.seed(seed)
    _w = jnp.asarray

    def _L0_attn_setup():
        import jax, jax.numpy as jnp
        import numpy as np
        B, T, D = (4, 512, 128)
        EPS = 1e-06
        key = jax.random.key(seed)
        ks = jax.random.split(key, 9)
        s = 0.02
        f32 = jnp.float32
        return {'x_seq': jax.random.normal(ks[0], (B, T, D), f32), 'W_q': jax.random.normal(ks[1], (D, D), f32) * s, 'b_q': jax.random.normal(ks[2], (D,), f32) * s, 'W_k': jax.random.normal(ks[3], (D, D), f32) * s, 'b_k': jax.random.normal(ks[4], (D,), f32) * s, 'W_v': jax.random.normal(ks[5], (D, D), f32) * s, 'b_v': jax.random.normal(ks[6], (D,), f32) * s, 'W_a': jax.random.normal(ks[7], (D, D), f32) * s, 'b_a': jax.random.normal(ks[8], (D,), f32) * s}
    _L0_attn_in = _L0_attn_setup()

    def _L0_ffn_setup():
        import jax, jax.numpy as jnp
        import numpy as np
        B, S, D, H, E, K = (4, 128, 128, 256, 8, 2)
        key = jax.random.key(seed)
        ks = jax.random.split(key, 5)
        s = 0.02
        return {'x': jax.random.normal(ks[0], (B, S, D), jnp.float32), 'W1': jax.random.normal(ks[1], (E, H, D), jnp.float32) * s, 'b1': jnp.zeros((E, H), jnp.float32), 'W2': jax.random.normal(ks[2], (E, D, H), jnp.float32) * s, 'b2': jnp.zeros((E, D), jnp.float32), 'Wg': jax.random.normal(ks[3], (E, D), jnp.float32) * s, 'bg': jnp.zeros((E,), jnp.float32)}
    _L0_ffn_in = _L0_ffn_setup()
    _L0_c = _w((lambda *s: np.random.randn(*s).astype(np.float32) * 0.05)(16, 128))
    _L0_wmod = _w((lambda *s: np.random.randn(*s).astype(np.float32) * 0.05)(128, 6 * 128) * 128 ** (-0.5))
    _d = {'L0_attn_x_seq': _L0_attn_in['x_seq'], 'L0_attn_W_q': _L0_attn_in['W_q'], 'L0_attn_b_q': _L0_attn_in['b_q'], 'L0_attn_W_k': _L0_attn_in['W_k'], 'L0_attn_b_k': _L0_attn_in['b_k'], 'L0_attn_W_v': _L0_attn_in['W_v'], 'L0_attn_b_v': _L0_attn_in['b_v'], 'L0_attn_W_a': _L0_attn_in['W_a'], 'L0_attn_b_a': _L0_attn_in['b_a'], 'L0_ffn_W1': _L0_ffn_in['W1'], 'L0_ffn_b1': _L0_ffn_in['b1'], 'L0_ffn_W2': _L0_ffn_in['W2'], 'L0_ffn_b2': _L0_ffn_in['b2'], 'L0_ffn_Wg': _L0_ffn_in['Wg'], 'L0_ffn_bg': _L0_ffn_in['bg'], 'L0_c': _L0_c, 'L0_wmod': _L0_wmod}
    _x0 = _d['L0_attn_x_seq']
    _d['L0_attn_x_seq'] = jax.random.normal(jax.random.fold_in(jax.random.key(seed), 1), (16, 256, 128), dtype=_x0.dtype)
    del _x0
    return _d

def reference(L0_attn_x_seq, L0_attn_W_q, L0_attn_b_q, L0_attn_W_k, L0_attn_b_k, L0_attn_W_v, L0_attn_b_v, L0_attn_W_a, L0_attn_b_a, L0_ffn_W1, L0_ffn_b1, L0_ffn_W2, L0_ffn_b2, L0_ffn_Wg, L0_ffn_bg, L0_c, L0_wmod):

    def _L0_attn_ref(x_seq, W_q, b_q, W_k, b_k, W_v, b_v, W_a, b_a):
        import jax, jax.numpy as jnp
        import numpy as np
        B, T, D = (4, 512, 128)
        EPS = 1e-06
        q = jax.nn.relu(x_seq @ W_q.T + b_q)
        k = jax.nn.relu(x_seq @ W_k.T + b_k)
        v = x_seq @ W_v.T + b_v
        A = jax.nn.sigmoid(x_seq @ W_a.T + b_a)
        log_g = jax.lax.cumsum(jnp.log(A + 1e-06), axis=1, reverse=True)
        wk = k * jnp.exp(log_g)
        scores = jnp.einsum('btd,bsd->bts', q, wk)
        Tn = x_seq.shape[1]
        mask = jnp.tril(jnp.ones((Tn, Tn), bool))
        scores = jnp.where(mask, scores, 0.0)
        num = jnp.einsum('bts,bsd->btd', scores, v)
        denom = scores.sum(-1, keepdims=True) + EPS
        return num / denom

    def _L0_ffn_ref(x, W1, b1, W2, b2, Wg, bg):
        import jax, jax.numpy as jnp
        import numpy as np
        B, S, D, H, E, K = (4, 128, 128, 256, 8, 2)
        b, s, d = x.shape
        xt = x.reshape(-1, d)
        gate_logits = xt @ Wg.T + bg
        w, idx = jax.lax.top_k(gate_logits, K)
        w = jax.nn.softmax(w, axis=1)
        h = jax.nn.relu(jnp.einsum('td,ehd->eth', xt, W1) + b1[:, None, :])
        y = jnp.einsum('eth,eoh->eto', h, W2) + b2[:, None, :]
        comb = (jax.nn.one_hot(idx, E, dtype=xt.dtype) * w[..., None]).sum(axis=1)
        out = jnp.einsum('eto,te->to', y, comb)
        return out.reshape(b, s, d)
    x = L0_attn_x_seq
    mod = (_silu(L0_c) @ L0_wmod).reshape(L0_c.shape[0], 6, 1, -1)
    sa, ca, ga, sb, cb, gb = (mod[:, 0], mod[:, 1], mod[:, 2], mod[:, 3], mod[:, 4], mod[:, 5])
    ga = (2 * (ga >= 0) - 1) * jnp.maximum(jnp.abs(ga), 0.25)
    gb = (2 * (gb >= 0) - 1) * jnp.maximum(jnp.abs(gb), 0.25)
    h = _layernorm(x, axis=-1) * (1 + ca) + sa
    x = x + ga * _L0_attn_ref(h, L0_attn_W_q, L0_attn_b_q, L0_attn_W_k, L0_attn_b_k, L0_attn_W_v, L0_attn_b_v, L0_attn_W_a, L0_attn_b_a)
    h = _layernorm(x, axis=-1) * (1 + cb) + sb
    x = x + gb * _L0_ffn_ref(h, L0_ffn_W1, L0_ffn_b1, L0_ffn_W2, L0_ffn_b2, L0_ffn_Wg, L0_ffn_bg)
    return x

_drawn_inputs = setup_inputs


def setup_inputs(seed=0):
    import zlib

    import numpy as np

    out = dict(_drawn_inputs(seed))
    spreads = {'L0_ffn_b1': (0.0, 0.8), 'L0_ffn_b2': (0.0, 0.456), 'L0_ffn_bg': (0.0, 0.717)}
    factors = {'L0_attn_W_q': 8.0,
     'L0_attn_b_q': 48.165,
     'L0_attn_W_k': 8.0,
     'L0_attn_b_k': 60.669,
     'L0_attn_W_v': 6.253,
     'L0_attn_b_v': 8.0,
     'L0_attn_W_a': 8.0,
     'L0_attn_b_a': 8.0,
     'L0_ffn_W1': 7.168,
     'L0_ffn_W2': 5.469,
     'L0_ffn_Wg': 3.318}
    for name, (base, spread) in spreads.items():
        noise = np.random.default_rng([zlib.crc32(name.encode()), seed]).standard_normal(out[name].shape)
        drawn = base * np.exp(spread * noise) if base else spread * noise
        out[name] = jnp.asarray(drawn.astype(out[name].dtype))
    for name, factor in factors.items():
        out[name] = (out[name] * factor).astype(out[name].dtype)
    return out
```

```python
from contextlib import ExitStack

import concourse.bass as bass
from concourse import mybir

F32 = mybir.dt.float32
F32R = mybir.dt.float32r
ALU = mybir.AluOpType
ACT = mybir.ActivationFunctionType
AX = mybir.AxisListType

P = 128
B, S, D = 16, 256, 128
E, H = 8, 256
HB = H // P
T = B * S
TG = 4 * P
G = T // TG
J = TG // P
BG = TG // S
JB = S // P
VW = D + 4
SC = S + P
LN_EPS = 1e-5
DEN_EPS = 1e-6
LOG_EPS = 1e-6
A_LEAST = -69.0
G_LEAST = 0.25


def adaln_block(nc, x, w_att, b_qka, b_v, w1t, b1t, w2t, b2, wgt, bg, ct, wmod, out, gate_rows):
    ctx = ExitStack()
    with ctx:
        def sb(name, shape, dt=F32):
            return ctx.enter_context(nc.sbuf_tensor(name, shape, dt))

        def sem(name):
            return ctx.enter_context(nc.semaphore(name))

        x_all = sb("x_all", [P, G * J, D])
        gates = sb("gates", [P, B, 2, D])
        mod = sb("mod", [P, 4, B])
        watt = sb("watt", [P, 4, D])
        watt_hi = sb("watt_hi", [P, 3, D], F32R)
        watt_lo = sb("watt_lo", [P, 3, D], F32R)
        w1 = sb("w1", [P, E * H])
        w1_hi = sb("w1_hi", [P, E * H], F32R)
        w1_lo = sb("w1_lo", [P, E * H], F32R)
        w2 = sb("w2", [P, E, HB, D])
        b1 = sb("b1", [P, E * HB])
        bqka = sb("bqka", [P, 3])
        bv = sb("bv", [P, D])
        wg = sb("wg", [P, E])
        bgate = sb("bgate", [P, E])
        b2d = sb("b2d", [J * E, J, D])
        ident = sb("ident", [P, P])
        causal = sb("causal", [P, SC])
        before = sb("before", [P, E, E])
        half_power = sb("half_power", [P, J])
        carrier = sb("carrier", [P, 1])
        log_bias = sb("log_bias", [P, 1])
        c_in = sb("c_in", [P, B])
        c_exp = sb("c_exp", [P, B])
        c_den = sb("c_den", [P, B])
        c_rec = sb("c_rec", [P, B])
        c_silu = sb("c_silu", [P, B])
        wm = sb("wm", [P, 6, D])
        g_raw = sb("g_raw", [B, 2 * D])
        g_neg = sb("g_neg", [B, 2 * D])
        g_mag = sb("g_mag", [B, 2 * D])
        g_sign = sb("g_sign", [B, 2 * D])
        g_out = sb("g_out", [B, 2 * D])
        stats = sb("stats", [P, J, 6])
        mv = sb("mv", [P, J, 2])
        var_eps = sb("var_eps", [P, J])
        rstd = sb("rstd", [P, J])
        xn = sb("xn", [P, J, D])
        mod_now = sb("mod_now", [P, 4, BG])
        h1 = sb("h1", [P, TG])
        h1_hi = sb("h1_hi", [P, TG], F32R)
        h1_lo = sb("h1_lo", [P, TG], F32R)
        h2 = sb("h2", [P, TG])
        h2_hi = sb("h2_hi", [P, TG], F32R)
        h2_lo = sb("h2_lo", [P, TG], F32R)
        a_in = sb("a_in", [P, TG])
        a_exp = sb("a_exp", [P, TG])
        a_up = sb("a_up", [P, TG])
        a_down = sb("a_down", [P, TG])
        log_g = sb("log_g", [P, TG])
        decay = sb("decay", [P, TG])
        qT = sb("qT", [P, TG])
        kT = sb("kT", [P, TG])
        wkT = sb("wkT", [P, TG])
        v = sb("v", [P, J, VW])
        scores = sb("scores", [P, BG, SC])
        den = sb("den", [P, J])
        rden = sb("rden", [P, J])
        att = sb("att", [P, J, D])
        logits = sb("logits", [P, J, E])
        top = sb("top", [P, J, 8])
        gap = sb("gap", [P, J])
        p_gap = sb("p_gap", [P, J])
        p_sum = sb("p_sum", [P, J])
        share1 = sb("share1", [P, J])
        share2 = sb("share2", [P, J])
        larger = sb("larger", [P, J, E, E])
        equal = sb("equal", [P, J, E, E])
        rank = sb("rank", [P, J, E])
        comb1 = sb("comb1", [P, J, E])
        comb2 = sb("comb2", [P, J, E])
        comb = sb("comb", [P, J, E])
        combT = sb("combT", [J * E, P])
        relu = sb("relu", [P, 2, HB, TG])
        acc = sb("acc", [P, J, D])
        scaled = sb("scaled", [P, J, D])
        def bank(name):
            return ctx.enter_context(nc.psum_tensor(name, [P, 512], F32))

        z_ps = [bank("z0"), bank("z1")]
        y_ps = [bank("y0"), bank("y1")]
        bank_a, bank_b, bank_c, bank_d = bank("bank_a"), bank("bank_b"), bank("bank_c"), bank("bank_d")

        in_c, in_wmod, in_x0, in_watt, in_b2, in_w1, in_w2, in_rest = (
            sem(n) for n in ("in_c", "in_wmod", "in_x0", "in_watt", "in_b2", "in_w1", "in_w2", "in_rest"))
        in_bqka, in_b1, in_bv, in_bg, in_wg = (sem(n) for n in ("in_bqka", "in_b1", "in_bv", "in_bg", "in_wg"))
        pool_step, pool_const, b2_zero, v_ones = (sem(n) for n in ("pool_step", "pool_const", "b2_zero", "v_ones"))
        c_exp_done, silu_done, mod_mm, gate_mm, mod_ready, gate_step, g_ready, g_stored, g_loaded = (
            sem(n) for n in ("c_exp_done", "silu_done", "mod_mm", "gate_mm", "mod_ready", "gate_step", "g_ready",
                             "g_stored", "g_loaded"))
        watt_split, w1_split, once_step = sem("watt_split"), sem("w1_split"), sem("once_step")
        var1, rstd1, xn1, xn1_T, h1_act, h1_split = (
            sem(n) for n in ("var1", "rstd1", "xn1", "xn1_T", "h1_act", "h1_split"))
        a_mm, k_mm, q_mm, v_mm = sem("a_mm"), sem("k_mm"), sem("q_mm"), sem("v_mm")
        a_clamped, a_exp_done, a_logs, log_g_done, decay_done = (
            sem(n) for n in ("a_clamped", "a_exp_done", "a_logs", "log_g_done", "decay_done"))
        k_done, q_done, v_done, wk_done = sem("k_done"), sem("q_done"), sem("v_done"), sem("wk_done")
        s_mm, s_masked, av_mm = sem("s_mm"), sem("s_masked"), sem("av_mm")
        var2, rstd2, xn2, xn2_T, h2_act, h2_split = (
            sem(n) for n in ("var2", "rstd2", "xn2", "xn2_T", "h2_act", "h2_split"))
        logits_mm, gap_done, gap_exp, comb_done, comb_T, combT_done, b2_mm = (
            sem(n) for n in ("logits_mm", "gap_done", "gap_exp", "comb_done", "comb_T", "combT_done", "b2_mm"))
        z_mm, relu_done, y_mm, acc_step, acc_free, result, stored = (
            sem(n) for n in ("z_mm", "relu_done", "y_mm", "acc_step", "acc_free", "result", "stored"))
        att_step, route_step, rank_done, comb1_done = (
            sem(n) for n in ("att_step", "route_step", "rank_done", "comb1_done"))

        B2_AFTER = 2
        ACC_STEPS = E * J + 1

        def acc_steps(e):
            return (e + 1) * J + (e > B2_AFTER)

        x_dram = x.rearrange("(n p) d -> p n d", p=P)
        out_dram = out.rearrange("(n p) d -> p n d", p=P)

        block = ctx.enter_context(nc.Block())

        @block.sync
        def _(sp):
            sp.dma_start(c_in[:], ct).then_inc(in_c, 16)
            sp.dma_start(x_all[:, 0:J, :], x_dram[:, 0:J, :]).then_inc(in_x0, 16)
            sp.dma_start(watt[:].rearrange("p m n -> p (m n)"), w_att).then_inc(in_watt, 16)
            sp.dma_start(w1[:], w1t).then_inc(in_w1, 16)
            sp.dma_start(x_all[:, J:G * J, :], x_dram[:, J:G * J, :]).then_inc(in_rest, 16)
            sp.dma_start(w2[:].rearrange("p e h n -> p (e h n)"), w2t).then_inc(in_w2, 16)
            sp.wait_ge(g_ready, 1)
            sp.dma_start(gate_rows, g_out[:]).then_inc(g_stored, 16)
            sp.wait_ge(g_stored, 16)
            sp.dma_start(gates[:].rearrange("p b m n -> p (b m n)"),
                         gate_rows.rearrange("b n -> (b n)").partition_broadcast(P)).then_inc(g_loaded, 16)
            with sp.Fori(0, G) as g:
                sp.wait_ge(result, g + 1)
                sp.dma_start(out_dram[:, bass.ts(g, J), :], x_all[:, bass.ts(g, J), :]).then_inc(stored, 16)
            sp.wait_ge(stored, 16 * G)

        @block.gpsimd
        def _(pool):
            nc.gpsimd.memset(b2d[:], 0.0).then_inc(b2_zero, 1)
            nc.gpsimd.memset(ident[:], 1.0).then_inc(pool_step, 1)
            nc.gpsimd.memset(causal[:], 1.0).then_inc(pool_step, 1)
            nc.gpsimd.memset(before[:], 1.0).then_inc(pool_step, 1)
            nc.gpsimd.memset(half_power[:], -0.5).then_inc(pool_const, 1)
            nc.gpsimd.memset(log_bias[:], 1.0 + LOG_EPS).then_inc(pool_const, 1)
            nc.gpsimd.memset(v[:], 1.0).then_inc(v_ones, 1)
            nc.gpsimd.memset(scaled[:], 0.0).then_inc(acc_free, 1)
            pool.wait_ge(pool_step, 3)
            nc.gpsimd.affine_select(out=ident[:], in_=ident[:], compare_op=ALU.is_equal, fill=0.0, base=0,
                                    pattern=[[1, P]], channel_multiplier=-1).then_inc(pool_const, 1)
            for first in (0, S):
                nc.gpsimd.affine_select(out=causal[:, first:first + P], in_=causal[:, first:first + P],
                                        compare_op=ALU.is_ge, fill=0.0, base=0,
                                        pattern=[[1, P]], channel_multiplier=-1).then_inc(pool_const, 1)
            nc.gpsimd.affine_select(out=before[:], in_=before[:], compare_op=ALU.is_gt, fill=0.0, base=0,
                                    pattern=[[1, E], [-1, E]], channel_multiplier=0).then_inc(pool_const, 1)

            def rstd_of(g, var_ready, rstd_done):
                pool.wait_ge(var_ready, g + 1)
                nc.gpsimd.tensor_tensor(rstd[:], var_eps[:], half_power[:], ALU.pow).then_inc(rstd_done, 1)

            def finish(g):
                pool.wait_ge(acc_step, ACC_STEPS * (g + 1))
                nc.gpsimd.tensor_tensor(scaled[:].rearrange("p (b j) d -> p b j d", b=BG),
                                        acc[:].rearrange("p (b j) d -> p b j d", b=BG),
                                        gates[:, bass.ts(g, BG), 1, :].unsqueeze(2).to_broadcast([P, BG, JB, D]),
                                        ALU.mult).then_inc(acc_free, 1)
                pool.wait_ge(acc_free, g + 2)
                nc.gpsimd.tensor_tensor(x_all[:, bass.ts(g, J), :], scaled[:], x_all[:, bass.ts(g, J), :],
                                        ALU.add).then_inc(result, 1)
                pool.wait_ge(result, g + 1)

            pool.wait_ge(pool_const, 6)
            rstd_of(0, var1, rstd1)
            rstd_of(0, var2, rstd2)
            pool.wait_ge(g_loaded, 16)
            with pool.Fori(0, G - 1) as g:
                rstd_of(g + 1, var1, rstd1)
                rstd_of(g + 1, var2, rstd2)
                finish(g)
            finish(G - 1)

        @block.scalar
        def _(act):
            act.dma_start(wm[:].rearrange("p m n -> p (m n)"), wmod).then_inc(in_wmod, 16)
            act.dma_start(bqka[:], b_qka).then_inc(in_bqka, 16)
            act.dma_start(bv[:], b_v.partition_broadcast(P)).then_inc(in_bv, 16)
            act.dma_start(b1[:], b1t).then_inc(in_b1, 16)
            act.dma_start(bgate[:], bg.partition_broadcast(P)).then_inc(in_bg, 16)
            act.dma_start(wg[:], wgt).then_inc(in_wg, 16)
            act.wait_ge(in_c, 16)
            nc.scalar.activation(c_exp[:], c_in[:], ACT.Exp, scale=-1.0).then_inc(c_exp_done, 1)
            act.wait_ge(b2_zero, 1)
            for j in range(J):
                act.dma_start(b2d[E * j:E * (j + 1), j, :], b2).then_inc(in_b2, 16)

            def modulate(dst, src, shift, done):
                for b in range(BG):
                    nc.scalar.activation(dst[:, b * S:(b + 1) * S], src[:, b * S:(b + 1) * S], ACT.Identity,
                                         scale=mod_now[:, shift + 1, b:b + 1],
                                         bias=mod_now[:, shift, b:b + 1]).then_inc(done, 1)

            def h1_of(g):
                act.wait_ge(xn1_T, g + 1)
                modulate(h1, bank_a, 0, h1_act)

            def a_of(g):
                act.wait_ge(a_clamped, g + 1)
                nc.scalar.activation(a_exp[:], a_in[:], ACT.Exp, scale=-1.0).then_inc(a_exp_done, 1)
                act.wait_ge(a_exp_done, g + 1)
                nc.scalar.activation(a_up[:], a_exp[:], ACT.Ln, scale=LOG_EPS, bias=log_bias[:]).then_inc(a_logs, 1)
                nc.scalar.activation(a_down[:], a_exp[:], ACT.Ln, scale=1.0, bias=1.0).then_inc(a_logs, 1)

            def k_of(g):
                act.wait_ge(k_mm, g + 1)
                nc.scalar.activation(kT[:], bank_c[:], ACT.Relu, bias=bqka[:, 1:2]).then_inc(k_done, 1)

            def q_of(g):
                act.wait_ge(q_mm, g + 1)
                nc.scalar.activation(qT[:], bank_d[:], ACT.Relu, bias=bqka[:, 0:1]).then_inc(q_done, 1)

            def decay_of(g):
                act.wait_ge(log_g_done, BG * (g + 1))
                nc.scalar.activation(decay[:], log_g[:], ACT.Exp).then_inc(decay_done, 1)

            def h2_of(g):
                act.wait_ge(xn2_T, g + 1)
                modulate(h2, bank_b, 2, h2_act)

            def gap_of(g):
                act.wait_ge(gap_done, g + 1)
                nc.scalar.activation(p_gap[:], gap[:], ACT.Exp).then_inc(gap_exp, 1)

            def relu_of(g, e):
                for hb in range(HB):
                    act.wait_ge(z_mm, HB * (E * g + e) + hb + 1)
                    nc.scalar.activation(relu[:, e % 2, hb, :], z_ps[hb][:], ACT.Relu,
                                         bias=b1[:, HB * e + hb:HB * e + hb + 1]).then_inc(relu_done, 1)

            def experts(g, following):
                for e in range(E):
                    relu_of(g, e)
                    if e == 0:
                        gap_of(g)
                    if following and e == 1:
                        h1_of(g + 1)
                    if following and e == 2:
                        k_of(g + 1)
                        a_of(g + 1)
                    if following and e == 4:
                        q_of(g + 1)
                        decay_of(g + 1)
                if following:
                    h2_of(g + 1)

            act.wait_ge(in_bqka, 16)
            act.wait_ge(in_b1, 16)
            act.wait_ge(pool_const, 6)
            h1_of(0)
            k_of(0)
            a_of(0)
            q_of(0)
            decay_of(0)
            h2_of(0)
            with act.Fori(0, G - 1) as g:
                experts(g, True)
            experts(G - 1, False)

        ATT_STEPS = 4 * J + J + BG + 4
        ROUTE_STEPS = J + 9

        @block.vector
        def _(dve):
            once = [0]

            def after_once(instruction):
                once[0] += 1
                instruction.then_inc(once_step, 1)
                dve.wait_ge(once_step, once[0])

            dve.wait_ge(c_exp_done, 1)
            after_once(nc.vector.tensor_scalar_add(c_den[:], c_exp[:], 1.0))
            after_once(nc.vector.reciprocal(c_rec[:], c_den[:]))
            nc.vector.tensor_tensor(c_silu[:], c_in[:], c_rec[:], ALU.mult).then_inc(silu_done, 1)

            att_count, route_count = [0], [0]

            def att_signal(instruction):
                att_count[0] += 1
                instruction.then_inc(att_step, 1)

            def att_wait(g):
                dve.wait_ge(att_step, ATT_STEPS * g + att_count[0])

            def att_hold(g):
                att_wait(g)
                nc.vector.memset(carrier[:], 0.0)

            def route_signal(instruction):
                route_count[0] += 1
                instruction.then_inc(route_step, 1)

            def route_wait(g):
                dve.wait_ge(route_step, ROUTE_STEPS * g + route_count[0])

            def statistics(g, var_ready):
                for j in range(J):
                    att_signal(nc.vector.bn_stats(stats[:, j, :], x_all[:, g * J + j, :]))
                att_hold(g)
                for j in range(J):
                    att_signal(nc.vector.bn_aggr(mv[:, j, :], stats[:, j, :]))
                att_wait(g)
                nc.vector.tensor_scalar_add(var_eps[:], mv[:, :, 1], LN_EPS).then_inc(var_ready, 1)

            def normalise(g, rstd_ready, done):
                dve.wait_ge(rstd_ready, g + 1)
                for j in range(J):
                    nc.vector.tensor_scalar(xn[:, j, :], x_all[:, g * J + j, :], mv[:, j, 0:1], rstd[:, j:j + 1],
                                            ALU.subtract, ALU.mult).then_inc(done, 1)

            def first_norm(g):
                att_count[0] = 0
                att_signal(nc.vector.tensor_copy(mod_now[:], mod[:, :, bass.ts(g, BG)]))
                statistics(g, var1)

            def split_h1(g):
                dve.wait_ge(h1_act, BG * (g + 1))
                att_signal(nc.vector.tensor_copy(h1_hi[:], h1[:]))
                att_wait(g)
                nc.vector.tensor_tensor(h1_lo[:], h1[:], h1_hi[:].bitcast(F32), ALU.subtract).then_inc(h1_split, 1)

            def clamp_a(g):
                dve.wait_ge(a_mm, g + 1)
                nc.vector.tensor_scalar(a_in[:], bank_b[:], bqka[:, 2:3], A_LEAST, ALU.add,
                                        ALU.max).then_inc(a_clamped, 1)

            def v_of(g):
                dve.wait_ge(v_mm, g + 1)
                nc.vector.tensor_tensor(v[:, :, 0:D], bank_a[:].rearrange("p (j d) -> p j d", j=J),
                                        bv[:].unsqueeze(1).to_broadcast([P, J, D]), ALU.add).then_inc(v_done, 1)

            def sum_logs(g):
                dve.wait_ge(a_logs, 2 * (g + 1))
                for b in range(BG):
                    back = slice(b * S + S - 1, b * S - 1 if b else None, -1)
                    nc.vector.tensor_tensor_scan(log_g[:, back], a_up[:, back], a_down[:, back], 0.0,
                                                 ALU.add, ALU.subtract).then_inc(log_g_done, 1)

            def decay_k(g):
                dve.wait_ge(decay_done, g + 1)
                dve.wait_ge(k_done, g + 1)
                nc.vector.tensor_tensor(wkT[:], kT[:], decay[:], ALU.mult).then_inc(wk_done, 1)

            def mask_scores(g):
                for b, ps in enumerate((bank_b, bank_c)):
                    dve.wait_ge(s_mm, BG * g + b + 1)
                    nc.vector.tensor_tensor(scores[:, b, :], ps[:, 0:SC], causal[:], ALU.mult).then_inc(s_masked, 1)

            def add_attention(g):
                for b, ps in enumerate((bank_d, bank_a)):
                    dve.wait_ge(av_mm, BG * g + b + 1)
                    att_signal(nc.vector.tensor_scalar_add(
                        den[:, b * JB:(b + 1) * JB], ps[:].rearrange("p (j n) -> p j n", j=JB)[:, :, D], DEN_EPS))
                att_wait(g)
                att_signal(nc.vector.reciprocal(rden[:], den[:]))
                att_wait(g)
                for b, ps in enumerate((bank_d, bank_a)):
                    for j in range(JB):
                        t = b * JB + j
                        att_signal(nc.vector.scalar_tensor_tensor(
                            out=att[:, t, :], in0=ps[:, j * S:j * S + D], scalar=rden[:, t:t + 1],
                            in1=gates[:, g * BG + b, 0, :], op0=ALU.mult, op1=ALU.mult))
                att_wait(g)
                att_signal(nc.vector.tensor_tensor(x_all[:, bass.ts(g, J), :], x_all[:, bass.ts(g, J), :], att[:],
                                                   ALU.add))
                att_hold(g)
                statistics(g, var2)
                assert att_count[0] == ATT_STEPS, att_count

            def split_h2(g):
                dve.wait_ge(h2_act, BG * (g + 1))
                nc.vector.tensor_copy(h2_hi[:], h2[:]).then_inc(h2_split, 1)
                dve.wait_ge(h2_split, 2 * g + 1)
                nc.vector.tensor_tensor(h2_lo[:], h2[:], h2_hi[:].bitcast(F32), ALU.subtract).then_inc(h2_split, 1)

            def route(g):
                route_count[0] = 0
                dve.wait_ge(logits_mm, g + 1)
                route_signal(nc.vector.tensor_tensor(logits[:], bank_c[:, 0:J * E].rearrange("p (j e) -> p j e", j=J),
                                                     bgate[:].unsqueeze(1).to_broadcast([P, J, E]), ALU.add))
                route_wait(g)
                one = logits[:].unsqueeze(3).to_broadcast([P, J, E, E])
                other = logits[:].unsqueeze(2).to_broadcast([P, J, E, E])
                route_signal(nc.vector.tensor_tensor(equal[:], other, one, ALU.is_equal))
                for j in range(J):
                    route_signal(nc.vector.max(top[:, j, :], logits[:, j, :]))
                route_wait(g)
                nc.vector.tensor_tensor(gap[:], top[:, :, 1], top[:, :, 0], ALU.subtract).then_inc(gap_done, 1)
                route_signal(nc.vector.tensor_tensor(
                    equal[:], equal[:], before[:].unsqueeze(1).to_broadcast([P, J, E, E]), ALU.mult))
                route_signal(nc.vector.tensor_tensor(larger[:], other, one, ALU.is_gt))
                route_wait(g)
                route_signal(nc.vector.tensor_tensor(larger[:], larger[:], equal[:], ALU.add))
                route_wait(g)
                dve.wait_ge(gap_exp, g + 1)
                nc.vector.tensor_reduce(rank[:], larger[:], AX.X, ALU.add).then_inc(rank_done, 1)
                route_signal(nc.vector.tensor_scalar_add(p_sum[:], p_gap[:], 1.0))
                route_wait(g)
                route_signal(nc.vector.reciprocal(share1[:], p_sum[:]))
                route_wait(g)
                route_signal(nc.vector.tensor_tensor(share2[:], p_gap[:], share1[:], ALU.mult))
                dve.wait_ge(rank_done, g + 1)
                nc.vector.scalar_tensor_tensor(
                    out=comb1[:], in0=rank[:], scalar=0.0, in1=share1[:].unsqueeze(2).to_broadcast([P, J, E]),
                    op0=ALU.is_equal, op1=ALU.mult).then_inc(comb1_done, 1)
                route_wait(g)
                route_signal(nc.vector.scalar_tensor_tensor(
                    out=comb2[:], in0=rank[:], scalar=1.0, in1=share2[:].unsqueeze(2).to_broadcast([P, J, E]),
                    op0=ALU.is_equal, op1=ALU.mult))
                route_wait(g)
                dve.wait_ge(comb1_done, g + 1)
                nc.vector.tensor_tensor(comb[:], comb1[:], comb2[:], ALU.add).then_inc(comb_done, 1)
                assert route_count[0] == ROUTE_STEPS, route_count

            def copy_combT(g):
                dve.wait_ge(comb_T, g + 1)
                nc.vector.tensor_copy(combT[:], bank_d[0:J * E, 0:P]).then_inc(combT_done, 1)

            def add_expert(g, e):
                dve.wait_ge(y_mm, E * g + e + 1)
                y = y_ps[e % 2][:].rearrange("p (j d) -> p j d", j=J)
                if e == 0:
                    dve.wait_ge(comb_done, g + 1)
                    dve.wait_ge(acc_free, g + 1)
                if e == B2_AFTER + 1:
                    dve.wait_ge(acc_step, ACC_STEPS * g + acc_steps(B2_AFTER) + 1)
                for j in range(J):
                    weight = comb[:, j, e:e + 1]
                    if e == 0:
                        nc.vector.tensor_scalar(acc[:, j, :], y[:, j, :], weight, None, ALU.mult).then_inc(acc_step, 1)
                        continue
                    if e != B2_AFTER + 1:
                        dve.wait_ge(acc_step, ACC_STEPS * g + acc_steps(e - 1) - J + j + 1)
                    nc.vector.scalar_tensor_tensor(out=acc[:, j, :], in0=y[:, j, :], scalar=weight,
                                                   in1=acc[:, j, :], op0=ALU.mult,
                                                   op1=ALU.add).then_inc(acc_step, 1)

            def add_b2(g):
                dve.wait_ge(b2_mm, g + 1)
                dve.wait_ge(acc_step, ACC_STEPS * g + acc_steps(B2_AFTER))
                nc.vector.tensor_tensor(acc[:].rearrange("p j d -> p (j d)"), bank_d[:],
                                        acc[:].rearrange("p j d -> p (j d)"), ALU.add).then_inc(acc_step, 1)

            def experts(g, following):
                if following:
                    first_norm(g + 1)
                route(g)
                if following:
                    normalise(g + 1, rstd1, xn1)
                add_expert(g, 0)
                copy_combT(g)
                if following:
                    split_h1(g + 1)
                add_expert(g, 1)
                if following:
                    clamp_a(g + 1)
                add_expert(g, 2)
                add_b2(g)
                if following:
                    v_of(g + 1)
                    sum_logs(g + 1)
                add_expert(g, 3)
                if following:
                    decay_k(g + 1)
                add_expert(g, 4)
                if following:
                    mask_scores(g + 1)
                    add_attention(g + 1)
                add_expert(g, 5)
                if following:
                    normalise(g + 1, rstd2, xn2)
                add_expert(g, 6)
                if following:
                    split_h2(g + 1)
                add_expert(g, 7)

            dve.wait_ge(in_watt, 16)
            after_once(nc.vector.tensor_copy(watt_hi[:], watt[:, 0:3, :]))
            nc.vector.tensor_tensor(watt_lo[:], watt[:, 0:3, :], watt_hi[:].bitcast(F32),
                                    ALU.subtract).then_inc(watt_split, 1)
            dve.wait_ge(mod_mm, 1)
            mod_ps = z_ps[0][:, 0:4 * B].rearrange("p (m b) -> p m b", m=4)
            nc.vector.tensor_copy(mod[:, 0:3:2, :], mod_ps[:, 0:3:2, :]).then_inc(mod_ready, 1)
            nc.vector.tensor_scalar_add(mod[:, 1:4:2, :], mod_ps[:, 1:4:2, :], 1.0).then_inc(mod_ready, 1)
            dve.wait_ge(gate_mm, 1)
            g_ps = y_ps[0][0:B, 0:2 * D]
            after_once(nc.vector.tensor_copy(g_raw[:], g_ps))
            nc.vector.tensor_scalar(g_sign[:], g_raw[:], 0.0, 2.0, ALU.is_ge, ALU.mult).then_inc(gate_step, 1)
            after_once(nc.vector.scalar_tensor_tensor(out=g_neg[:], in0=g_raw[:], scalar=-1.0, in1=g_raw[:],
                                                      op0=ALU.mult, op1=ALU.max))
            after_once(nc.vector.tensor_scalar_max(g_mag[:], g_neg[:], G_LEAST))
            dve.wait_ge(gate_step, 1)
            nc.vector.scalar_tensor_tensor(out=g_out[:], in0=g_sign[:], scalar=-1.0, in1=g_mag[:],
                                           op0=ALU.add, op1=ALU.mult).then_inc(g_ready, 1)

            dve.wait_ge(mod_ready, 2)
            dve.wait_ge(in_x0, 16)
            first_norm(0)
            normalise(0, rstd1, xn1)
            split_h1(0)
            dve.wait_ge(in_bqka, 16)
            clamp_a(0)
            dve.wait_ge(in_bv, 16)
            dve.wait_ge(v_ones, 1)
            v_of(0)
            sum_logs(0)
            dve.wait_ge(in_w1, 16)
            after_once(nc.vector.tensor_copy(w1_hi[:], w1[:]))
            nc.vector.tensor_tensor(w1_lo[:], w1[:], w1_hi[:].bitcast(F32), ALU.subtract).then_inc(w1_split, 1)
            decay_k(0)
            dve.wait_ge(pool_const, 6)
            mask_scores(0)
            dve.wait_ge(g_loaded, 16)
            add_attention(0)
            normalise(0, rstd2, xn2)
            split_h2(0)
            dve.wait_ge(in_bg, 16)
            dve.wait_ge(in_rest, 16)
            with dve.Fori(0, G - 1) as g:
                experts(g, True)
            experts(G - 1, False)

        @block.tensor
        def _(pe):
            def mm(dst, lhsT, rhs, start=True, stop=True):
                return nc.tensor.matmul(dst, lhsT, rhs, start=start, stop=stop)

            def in_halves(dst, w_hi, w_lo, m_hi, m_lo):
                mm(dst, w_hi, m_hi, stop=False)
                mm(dst, w_hi, m_lo, start=False, stop=False)
                return mm(dst, w_lo, m_hi, start=False)

            def transpose_rows(g, ready, ps, done):
                pe.wait_ge(ready, J * (g + 1))
                for j in range(J):
                    last = nc.tensor.transpose(ps[:, j * P:(j + 1) * P], xn[:, j, :], ident[:])
                last.then_inc(done, 1)

            def a_and_k(g):
                pe.wait_ge(h1_split, g + 1)
                in_halves(bank_b[:], watt_hi[:, 2, :], watt_lo[:, 2, :], h1_hi[:], h1_lo[:]).then_inc(a_mm, 1)
                in_halves(bank_c[:], watt_hi[:, 1, :], watt_lo[:, 1, :], h1_hi[:], h1_lo[:]).then_inc(k_mm, 1)

            def v_of(g):
                for j in range(J):
                    last = mm(bank_a[:, j * D:(j + 1) * D], h1[:, j * P:(j + 1) * P], watt[:, 3, :])
                last.then_inc(v_mm, 1)

            def q_of(g):
                in_halves(bank_d[:], watt_hi[:, 0, :], watt_lo[:, 0, :], h1_hi[:], h1_lo[:]).then_inc(q_mm, 1)

            def scores_of(g):
                pe.wait_ge(wk_done, g + 1)
                pe.wait_ge(q_done, g + 1)
                for b, ps in enumerate((bank_b, bank_c)):
                    t0 = b * S
                    mm(ps[:, 0:S], wkT[:, t0:t0 + P], qT[:, t0:t0 + S])
                    mm(ps[:, S:SC], wkT[:, t0 + P:t0 + S], qT[:, t0 + P:t0 + S]).then_inc(s_mm, 1)

            def values_of(g):
                pe.wait_ge(v_done, g + 1)
                for b, ps in enumerate((bank_d, bank_a)):
                    pe.wait_ge(s_masked, BG * g + b + 1)
                    mm(ps[:, 0:D + 1], scores[:, b, 0:P], v[:, b * JB, 0:D + 1])
                    mm(ps[:, S:S + D + 1], scores[:, b, P:S], v[:, b * JB, 0:D + 1], stop=False)
                    mm(ps[:, S:S + D + 1], scores[:, b, S:SC], v[:, b * JB + 1, 0:D + 1],
                       start=False).then_inc(av_mm, 1)

            def logits_of(g):
                pe.wait_ge(h2_act, BG * (g + 1))
                for j in range(J):
                    last = mm(bank_c[:, j * E:(j + 1) * E], h2[:, j * P:(j + 1) * P], wg[:])
                last.then_inc(logits_mm, 1)

            def transpose_comb(g):
                pe.wait_ge(comb_done, g + 1)
                nc.tensor.transpose(bank_d[0:J * E, 0:P], comb[:].rearrange("p j e -> p (j e)"),
                                    ident[:]).then_inc(comb_T, 1)

            def b2_of(g):
                pe.wait_ge(combT_done, g + 1)
                mm(bank_d[:], combT[:], b2d[:].rearrange("k j d -> k (j d)")).then_inc(b2_mm, 1)

            def hidden(g, e):
                for hb in range(HB):
                    if e > 0:
                        pe.wait_ge(relu_done, HB * (E * g + e - 1) + hb + 1)
                    w = slice((HB * e + hb) * P, (HB * e + hb + 1) * P)
                    in_halves(z_ps[hb][:], w1_hi[:, w], w1_lo[:, w], h2_hi[:], h2_lo[:]).then_inc(z_mm, 1)

            def expert_out(g, e, following):
                pe.wait_ge(relu_done, HB * (E * g + e) + HB)
                if e >= 2:
                    pe.wait_ge(acc_step, ACC_STEPS * g + acc_steps(e - 2))
                elif not following:
                    pe.wait_ge(acc_step, ACC_STEPS * (g - 1) + acc_steps(e - 2 + E))
                for j in range(J):
                    for hb in range(HB):
                        last = mm(y_ps[e % 2][:, j * D:(j + 1) * D], relu[:, e % 2, hb, j * P:(j + 1) * P],
                                  w2[:, e, hb, :], start=hb == 0, stop=hb == HB - 1)
                last.then_inc(y_mm, 1)

            def experts(g, following):
                hidden(g, 0)
                hidden(g, 1)
                if following:
                    transpose_rows(g + 1, xn1, bank_a, xn1_T)
                expert_out(g, 0, following)
                hidden(g, 2)
                transpose_comb(g)
                if following:
                    a_and_k(g + 1)
                expert_out(g, 1, following)
                hidden(g, 3)
                b2_of(g)
                if following:
                    v_of(g + 1)
                expert_out(g, 2, following)
                hidden(g, 4)
                if following:
                    pe.wait_ge(acc_step, ACC_STEPS * g + acc_steps(B2_AFTER) + 1)
                    q_of(g + 1)
                expert_out(g, 3, following)
                hidden(g, 5)
                if following:
                    scores_of(g + 1)
                expert_out(g, 4, following)
                hidden(g, 6)
                if following:
                    values_of(g + 1)
                expert_out(g, 5, following)
                hidden(g, 7)
                if following:
                    transpose_rows(g + 1, xn2, bank_b, xn2_T)
                expert_out(g, 6, following)
                expert_out(g, 7, following)
                if following:
                    logits_of(g + 1)
                    pe.wait_ge(h2_split, 2 * (g + 2))

            pe.wait_ge(in_wmod, 16)
            pe.wait_ge(silu_done, 1)
            for i, chunk in enumerate((0, 1, 3, 4)):
                last = mm(z_ps[0][:, i * B:(i + 1) * B], wm[:, chunk, :], c_silu[:])
            last.then_inc(mod_mm, 1)
            for i, chunk in enumerate((2, 5)):
                last = mm(y_ps[0][0:B, i * D:(i + 1) * D], c_silu[:], wm[:, chunk, :])
            last.then_inc(gate_mm, 1)

            pe.wait_ge(pool_const, 6)
            transpose_rows(0, xn1, bank_a, xn1_T)
            pe.wait_ge(watt_split, 1)
            a_and_k(0)
            v_of(0)
            q_of(0)
            scores_of(0)
            values_of(0)
            transpose_rows(0, xn2, bank_b, xn2_T)
            pe.wait_ge(in_wg, 16)
            logits_of(0)
            pe.wait_ge(h2_split, 2)
            pe.wait_ge(w1_split, 1)
            pe.wait_ge(in_w2, 16)
            pe.wait_ge(in_b2, 16 * J)
            with pe.Fori(0, G - 1) as g:
                experts(g, True)
            experts(G - 1, False)


def kernel(**inputs):
    import numpy as np
    import concourse.bacc as bacc
    from concourse.bass_utils import run_bass_kernel_spmd

    def a(name):
        return np.asarray(inputs["L0_" + name])

    arrays = {
        "x": a("attn_x_seq").reshape(T, D),
        "w_att": np.concatenate([a(f"attn_W_{m}").T for m in "qkav"], axis=1),
        "b_qka": np.stack([a(f"attn_b_{m}") for m in "qka"], axis=1),
        "b_v": a("attn_b_v"),
        "w1t": a("ffn_W1").transpose(2, 0, 1).reshape(D, E * H),
        "b1t": a("ffn_b1").reshape(E * HB, P).T,
        "w2t": a("ffn_W2").reshape(E, D, HB, P).transpose(3, 0, 2, 1).reshape(P, E * HB * D),
        "b2": a("ffn_b2"),
        "wgt": a("ffn_Wg").T,
        "bg": a("ffn_bg"),
        "ct": a("c").T,
        "wmod": a("wmod"),
    }
    arrays = {name: np.ascontiguousarray(value) for name, value in arrays.items()}
    nc = bacc.Bacc("TRN2", target_bir_lowering=False, num_devices=1)
    args = {name: nc.dram_tensor(f"{name}_dram", value.shape, F32, kind="ExternalInput").ap()
            for name, value in arrays.items()}
    out = nc.dram_tensor("out_dram", (T, D), F32, kind="ExternalOutput").ap()
    gate_rows = nc.dram_tensor("gate_rows", (B, 2 * D), F32, kind="Internal").ap()
    adaln_block(nc, out=out, gate_rows=gate_rows, **args)
    got = run_bass_kernel_spmd(nc, [{f"{name}_dram": value for name, value in arrays.items()}], core_ids=[0])
    return got.results[0]["out_dram"].reshape(B, S, D)
```

```python
from contextlib import ExitStack

import concourse.bass as bass
from concourse import mybir

F32 = mybir.dt.float32
F32R = mybir.dt.float32r
ALU = mybir.AluOpType
ACT = mybir.ActivationFunctionType
AX = mybir.AxisListType

P = 128
B, S, D = 16, 256, 128
E, H = 8, 256
HB = H // P
T = B * S
TG = 4 * P
G = T // TG
J = TG // P
BG = TG // S
JB = S // P
VW = D + 4
SC = S + P
LN_EPS = 1e-5
DEN_EPS = 1e-6
LOG_EPS = 1e-6
A_LEAST = -69.0
G_LEAST = 0.25


def adaln_block(nc, x, w_att, b_qka, b_v, w1t, b1t, w2t, b2, wgt, bg, ct, wmod, out, gate_rows):
    ctx = ExitStack()
    with ctx:
        def sb(name, shape, dt=F32):
            return ctx.enter_context(nc.sbuf_tensor(name, shape, dt))

        def sem(name):
            return ctx.enter_context(nc.semaphore(name))

        x_all = sb("x_all", [P, G * J, D])
        gates = sb("gates", [P, B, 2, D])
        mod = sb("mod", [P, 4, B])
        watt = sb("watt", [P, 4, D])
        watt_hi = sb("watt_hi", [P, 3, D], F32R)
        watt_lo = sb("watt_lo", [P, 3, D], F32R)
        w1 = sb("w1", [P, E * H])
        w1_hi = sb("w1_hi", [P, E * H], F32R)
        w1_lo = sb("w1_lo", [P, E * H], F32R)
        w2 = sb("w2", [P, E, HB, D])
        b1 = sb("b1", [P, E * HB])
        bqka = sb("bqka", [P, 3])
        bv = sb("bv", [P, D])
        wg = sb("wg", [P, E])
        bgate = sb("bgate", [P, E])
        b2d = sb("b2d", [P, J, D])
        b2_halves = sb("b2_halves", [P, J, D], F32R)
        ident = sb("ident", [P, P])
        causal = sb("causal", [P, SC])
        before = sb("before", [P, E, E])
        half_power = sb("half_power", [P, J])
        carrier = sb("carrier", [P, 1])
        log_bias = sb("log_bias", [P, 1])
        c_in = sb("c_in", [P, B])
        c_exp = sb("c_exp", [P, B])
        c_den = sb("c_den", [P, B])
        c_rec = sb("c_rec", [P, B])
        c_silu = sb("c_silu", [P, B])
        wm = sb("wm", [P, 6, D])
        g_raw = sb("g_raw", [B, 2 * D])
        g_neg = sb("g_neg", [B, 2 * D])
        g_mag = sb("g_mag", [B, 2 * D])
        g_sign = sb("g_sign", [B, 2 * D])
        g_out = sb("g_out", [B, 2 * D])
        stats = sb("stats", [P, J, 6])
        mv = sb("mv", [P, J, 2])
        var_eps = sb("var_eps", [P, J])
        rstd = sb("rstd", [P, J])
        xn = sb("xn", [P, J, D])
        stats_in = sb("stats_in", [P, J, 6])
        mv_in = sb("mv_in", [P, J, 2])
        var_in = sb("var_in", [P, J])
        rstd_in = sb("rstd_in", [P, J])
        xn_in = sb("xn_in", [P, J, D])
        x2 = sb("x2", [P, J, D])
        mod_now = sb("mod_now", [P, 4, BG])
        h1 = sb("h1", [P, TG])
        h1_hi = sb("h1_hi", [P, TG], F32R)
        h1_lo = sb("h1_lo", [P, TG], F32R)
        h2 = sb("h2", [P, TG])
        h2_hi = sb("h2_hi", [P, TG], F32R)
        h2_lo = sb("h2_lo", [P, TG], F32R)
        a_in = sb("a_in", [P, TG])
        a_exp = sb("a_exp", [P, TG])
        a_up = sb("a_up", [P, TG])
        a_down = sb("a_down", [P, TG])
        log_g = sb("log_g", [P, TG])
        decay = sb("decay", [P, TG])
        qT = sb("qT", [P, TG])
        kT = sb("kT", [P, TG])
        wkT = sb("wkT", [P, TG])
        v = sb("v", [P, J, VW])
        scores = sb("scores", [P, BG, SC])
        den = sb("den", [P, J])
        rden = sb("rden", [P, J])
        logits = sb("logits", [P, J, E])
        top = sb("top", [P, J, 8])
        gap = sb("gap", [P, J])
        p_gap = sb("p_gap", [P, J])
        p_sum = sb("p_sum", [P, J])
        share1 = sb("share1", [P, J])
        share2 = sb("share2", [P, J])
        larger = sb("larger", [P, J, E, E])
        equal = sb("equal", [P, J, E, E])
        rank = sb("rank", [P, J, E])
        comb1 = sb("comb1", [P, J, E])
        comb2 = sb("comb2", [P, J, E])
        comb = sb("comb", [P, J, E])
        comb_hi = sb("comb_hi", [P, J * E], F32R)
        comb_halves = sb("comb_halves", [P, 4, J * E])
        combT = sb("combT", [P, P], F32R)
        relu = sb("relu", [P, 2, HB, TG])
        acc = sb("acc", [P, J, D])
        scaled = sb("scaled", [P, J, D])
        def bank(name):
            return ctx.enter_context(nc.psum_tensor(name, [P, 512], F32))

        z_ps = [bank("z0"), bank("z1")]
        y_ps = [bank("y0"), bank("y1")]
        bank_a, bank_b, bank_c, bank_d = bank("bank_a"), bank("bank_b"), bank("bank_c"), bank("bank_d")

        in_c, in_wmod, in_x0, in_watt, in_b2, in_w1, in_w2, in_rest = (
            sem(n) for n in ("in_c", "in_wmod", "in_x0", "in_watt", "in_b2", "in_w1", "in_w2", "in_rest"))
        in_bqka, in_b1, in_bv, in_bg, in_wg = (sem(n) for n in ("in_bqka", "in_b1", "in_bv", "in_bg", "in_wg"))
        pool_step, pool_const, b2_zero, v_ones = (sem(n) for n in ("pool_step", "pool_const", "b2_zero", "v_ones"))
        c_exp_done, silu_done, mod_mm, gate_mm, mod_ready, gate_step, g_ready, g_stored, g_loaded = (
            sem(n) for n in ("c_exp_done", "silu_done", "mod_mm", "gate_mm", "mod_ready", "gate_step", "g_ready",
                             "g_stored", "g_loaded"))
        watt_split, w1_split, once_step = sem("watt_split"), sem("w1_split"), sem("once_step")
        var1, rstd1, xn1, xn1_T, h1_act, h1_split = (
            sem(n) for n in ("var1", "rstd1", "xn1", "xn1_T", "h1_act", "h1_split"))
        a_mm, k_mm, q_mm, v_mm = sem("a_mm"), sem("k_mm"), sem("q_mm"), sem("v_mm")
        a_clamped, a_exp_done, a_logs, log_g_done, decay_done = (
            sem(n) for n in ("a_clamped", "a_exp_done", "a_logs", "log_g_done", "decay_done"))
        k_done, q_done, v_done, wk_done = sem("k_done"), sem("q_done"), sem("v_done"), sem("wk_done")
        s_mm, s_masked, av_mm = sem("s_mm"), sem("s_masked"), sem("av_mm")
        var2, rstd2, xn2, xn2_T, h2_act, h2_split = (
            sem(n) for n in ("var2", "rstd2", "xn2", "xn2_T", "h2_act", "h2_split"))
        logits_mm, gap_done, gap_exp, comb_done, comb_T, combT_done, b2_mm = (
            sem(n) for n in ("logits_mm", "gap_done", "gap_exp", "comb_done", "comb_T", "combT_done", "b2_mm"))
        z_mm, relu_done, y_mm, acc_step, acc_free, result, stored = (
            sem(n) for n in ("z_mm", "relu_done", "y_mm", "acc_step", "acc_free", "result", "stored"))
        mod_taken, v_gated, x2_kept, norm_step = (sem(n) for n in ("mod_taken", "v_gated", "x2_kept", "norm_step"))
        in_x1, halved, b2_split, last_rows, last_step = (
            sem(n) for n in ("in_x1", "halved", "b2_split", "last_rows", "last_step"))
        att_step, route_step, rank_done, comb1_done = (
            sem(n) for n in ("att_step", "route_step", "rank_done", "comb1_done"))

        B2_AFTER = 5
        ACC_STEPS = E * J + 1

        def acc_steps(e):
            return (e + 1) * J + (e > B2_AFTER)

        x_dram = x.rearrange("(n p) d -> p n d", p=P)
        out_dram = out.rearrange("(n p) d -> p n d", p=P)

        block = ctx.enter_context(nc.Block())

        @block.sync
        def _(sp):
            sp.dma_start(x_all[:, 0:J, :], x_dram[:, 0:J, :]).then_inc(in_x0, 16)
            sp.dma_start(watt[:].rearrange("p m n -> p (m n)"), w_att).then_inc(in_watt, 16)
            sp.dma_start(x_all[:, J:2 * J, :], x_dram[:, J:2 * J, :]).then_inc(in_x1, 16)
            sp.dma_start(w1[:], w1t).then_inc(in_w1, 16)
            sp.dma_start(w2[:].rearrange("p e h n -> p (e h n)"), w2t).then_inc(in_w2, 16)
            sp.dma_start(x_all[:, 2 * J:G * J, :], x_dram[:, 2 * J:G * J, :]).then_inc(in_rest, 16)
            sp.wait_ge(g_ready, 1)
            sp.dma_start(gate_rows, g_out[:]).then_inc(g_stored, 16)
            sp.wait_ge(g_stored, 16)
            sp.dma_start(gates[:].rearrange("p b m n -> p (b m n)"),
                         gate_rows.rearrange("b n -> (b n)").partition_broadcast(P)).then_inc(g_loaded, 16)
            with sp.Fori(0, G - 1) as g:
                sp.wait_ge(result, g + 1)
                sp.dma_start(out_dram[:, bass.ts(g, J), :], x_all[:, bass.ts(g, J), :]).then_inc(stored, 16)
            for b in range(BG):
                rows = slice((G - 1) * J + b * JB, (G - 1) * J + (b + 1) * JB)
                sp.wait_ge(last_rows, b + 1)
                sp.dma_start(out_dram[:, rows, :], x_all[:, rows, :]).then_inc(stored, 16)
            sp.wait_ge(stored, 16 * (G - 1 + BG))

        @block.gpsimd
        def _(pool):
            nc.gpsimd.memset(b2d[:], 0.0).then_inc(b2_zero, 1)
            nc.gpsimd.memset(ident[:], 1.0).then_inc(pool_step, 1)
            nc.gpsimd.memset(causal[:], 1.0).then_inc(pool_step, 1)
            nc.gpsimd.memset(before[:], 1.0).then_inc(pool_step, 1)
            nc.gpsimd.memset(half_power[:], -0.5).then_inc(pool_const, 1)
            nc.gpsimd.memset(log_bias[:], 1.0 + LOG_EPS).then_inc(pool_const, 1)
            nc.gpsimd.memset(v[:], 1.0).then_inc(v_ones, 1)
            nc.gpsimd.memset(scaled[:], 0.0).then_inc(acc_free, 1)
            pool.wait_ge(pool_step, 3)
            nc.gpsimd.affine_select(out=ident[:], in_=ident[:], compare_op=ALU.is_equal, fill=0.0, base=0,
                                    pattern=[[1, P]], channel_multiplier=-1).then_inc(pool_const, 1)
            for first in (0, S):
                nc.gpsimd.affine_select(out=causal[:, first:first + P], in_=causal[:, first:first + P],
                                        compare_op=ALU.is_ge, fill=0.0, base=0,
                                        pattern=[[1, P]], channel_multiplier=-1).then_inc(pool_const, 1)
            nc.gpsimd.affine_select(out=before[:], in_=before[:], compare_op=ALU.is_gt, fill=0.0, base=0,
                                    pattern=[[1, E], [-1, E]], channel_multiplier=0).then_inc(pool_const, 1)

            def rstd_of(g, var, var_ready, power, rstd_done):
                pool.wait_ge(var_ready, g + 1)
                nc.gpsimd.tensor_tensor(power[:], var[:], half_power[:], ALU.pow).then_inc(rstd_done, 1)

            def gate_of(g, which):
                return gates[:, bass.ts(g, BG), which, :].unsqueeze(2).to_broadcast([P, BG, JB, D])

            def gate_v(g):
                pool.wait_ge(v_done, g + 1)
                rows = v[:].rearrange("p (b j) d -> p b j d", b=BG)[:, :, :, 0:D]
                nc.gpsimd.tensor_tensor(rows, rows, gate_of(g, 0), ALU.mult).then_inc(v_gated, 1)

            def finish(g):
                pool.wait_ge(x2_kept, g + 1)
                pool.wait_ge(acc_step, ACC_STEPS * (g + 1))
                nc.gpsimd.tensor_tensor(scaled[:].rearrange("p (b j) d -> p b j d", b=BG),
                                        acc[:].rearrange("p (b j) d -> p b j d", b=BG), gate_of(g, 1),
                                        ALU.mult).then_inc(acc_free, 1)
                pool.wait_ge(acc_free, g + 2)
                nc.gpsimd.tensor_tensor(x_all[:, bass.ts(g, J), :], scaled[:], x_all[:, bass.ts(g, J), :],
                                        ALU.add).then_inc(result, 1)
                pool.wait_ge(result, g + 1)

            def experts(g, following, preparing):
                if following:
                    gate_v(g + 1)
                if preparing:
                    rstd_of(g + 2, var_in, var1, rstd_in, rstd1)
                if following:
                    rstd_of(g + 1, var_eps, var2, rstd, rstd2)
                if following:
                    finish(g)

            pool.wait_ge(pool_const, 6)
            rstd_of(0, var_in, var1, rstd_in, rstd1)
            pool.wait_ge(g_loaded, 16)
            gate_v(0)
            rstd_of(1, var_in, var1, rstd_in, rstd1)
            rstd_of(0, var_eps, var2, rstd, rstd2)
            with pool.Fori(0, G - 2) as g:
                experts(g, True, True)
            experts(G - 2, True, False)

        @block.scalar
        def _(act):
            act.dma_start(c_in[:], ct).then_inc(in_c, 16)
            act.dma_start(wm[:].rearrange("p m n -> p (m n)"), wmod).then_inc(in_wmod, 16)
            act.dma_start(bqka[:], b_qka).then_inc(in_bqka, 16)
            act.dma_start(bv[:], b_v.partition_broadcast(P)).then_inc(in_bv, 16)
            act.dma_start(b1[:], b1t).then_inc(in_b1, 16)
            act.dma_start(bgate[:], bg.partition_broadcast(P)).then_inc(in_bg, 16)
            act.dma_start(wg[:], wgt).then_inc(in_wg, 16)
            nc.scalar.preload_act_table_set("natural_log_exp_and_others")
            act.wait_ge(in_c, 16)
            nc.scalar.activation(c_exp[:], c_in[:], ACT.Exp, scale=-1.0).then_inc(c_exp_done, 1)
            act.wait_ge(b2_zero, 1)
            for k in range(P // E):
                act.dma_start(b2d[E * k:E * (k + 1), k % J, :], b2).then_inc(in_b2, 16)

            def modulate(dst, src, shift, done):
                for b in range(BG):
                    nc.scalar.activation(dst[:, b * S:(b + 1) * S], src[:, b * S:(b + 1) * S], ACT.Identity,
                                         scale=mod_now[:, shift + 1, b:b + 1],
                                         bias=mod_now[:, shift, b:b + 1]).then_inc(done, 1)

            def h1_of(g):
                act.wait_ge(mod_taken, g + 1)
                act.wait_ge(xn1_T, g + 1)
                modulate(h1, bank_a, 0, h1_act)

            def a_of(g):
                act.wait_ge(a_clamped, g + 1)
                nc.scalar.activation(a_exp[:], a_in[:], ACT.Exp, scale=-1.0).then_inc(a_exp_done, 1)
                act.wait_ge(a_exp_done, g + 1)
                nc.scalar.activation(a_up[:], a_exp[:], ACT.Ln, scale=LOG_EPS, bias=log_bias[:]).then_inc(a_logs, 1)
                nc.scalar.activation(a_down[:], a_exp[:], ACT.Ln, scale=1.0, bias=1.0).then_inc(a_logs, 1)

            def k_of(g):
                act.wait_ge(k_mm, g + 1)
                nc.scalar.activation(kT[:], bank_c[:], ACT.Relu, bias=bqka[:, 1:2]).then_inc(k_done, 1)

            def q_of(g):
                act.wait_ge(q_mm, g + 1)
                nc.scalar.activation(qT[:], bank_d[:], ACT.Relu, bias=bqka[:, 0:1]).then_inc(q_done, 1)

            def decay_of(g):
                act.wait_ge(log_g_done, BG * (g + 1))
                nc.scalar.activation(decay[:], log_g[:], ACT.Exp).then_inc(decay_done, 1)

            def h2_of(g):
                act.wait_ge(xn2_T, g + 1)
                modulate(h2, bank_b, 2, h2_act)
                nc.scalar.copy(x_all[:, bass.ts(g, J), :], x2[:]).then_inc(x2_kept, 1)

            def gap_of(g):
                act.wait_ge(gap_done, g + 1)
                nc.scalar.activation(p_gap[:], gap[:], ACT.Exp).then_inc(gap_exp, 1)

            def relu_of(g, e):
                for hb in range(HB):
                    act.wait_ge(z_mm, HB * (E * g + e) + hb + 1)
                    nc.scalar.activation(relu[:, e % 2, hb, :], z_ps[hb][:], ACT.Relu,
                                         bias=b1[:, HB * e + hb:HB * e + hb + 1]).then_inc(relu_done, 1)

            def experts(g, following):
                for e in range(E):
                    relu_of(g, e)
                    if e == 0:
                        gap_of(g)
                        if following:
                            h1_of(g + 1)
                    if following and e == 2:
                        a_of(g + 1)
                        k_of(g + 1)
                    if following and e == 3:
                        q_of(g + 1)
                        decay_of(g + 1)
                    if following and e == E - 1:
                        h2_of(g + 1)

            act.wait_ge(in_bqka, 16)
            act.wait_ge(in_b1, 16)
            act.wait_ge(pool_const, 6)
            h1_of(0)
            a_of(0)
            k_of(0)
            q_of(0)
            decay_of(0)
            h2_of(0)
            with act.Fori(0, G - 1) as g:
                experts(g, True)
            experts(G - 1, False)

        ATT_STEPS = 2 * J + J + BG + 2
        NORM_STEPS = 2 * J
        ROUTE_STEPS = J + 9

        @block.vector
        def _(dve):
            once = [0]

            def after_once(instruction):
                once[0] += 1
                instruction.then_inc(once_step, 1)
                dve.wait_ge(once_step, once[0])

            att_count, route_count = [0], [0]

            def att_signal(instruction):
                att_count[0] += 1
                instruction.then_inc(att_step, 1)

            def att_wait(g):
                dve.wait_ge(att_step, ATT_STEPS * g + att_count[0])

            def att_hold(g):
                att_wait(g)
                nc.vector.memset(carrier[:], 0.0)

            def route_signal(instruction):
                route_count[0] += 1
                instruction.then_inc(route_step, 1)

            def route_wait(g):
                dve.wait_ge(route_step, ROUTE_STEPS * g + route_count[0])

            def normalise(g, rows, at, mean_var, power, rstd_ready, dst, done):
                dve.wait_ge(rstd_ready, g + 1)
                for j in range(J):
                    nc.vector.tensor_scalar(dst[:, j, :], rows[:, at + j, :], mean_var[:, j, 0:1], power[:, j:j + 1],
                                            ALU.subtract, ALU.mult).then_inc(done, 1)

            def measure_in(g):
                for j in range(J):
                    nc.vector.bn_stats(stats_in[:, j, :], x_all[:, g * J + j, :]).then_inc(norm_step, 1)
                dve.wait_ge(norm_step, NORM_STEPS * g + J)
                nc.vector.memset(carrier[:], 0.0)
                for j in range(J):
                    nc.vector.bn_aggr(mv_in[:, j, :], stats_in[:, j, :]).then_inc(norm_step, 1)
                dve.wait_ge(norm_step, NORM_STEPS * (g + 1))
                nc.vector.tensor_scalar_add(var_in[:], mv_in[:, :, 1], LN_EPS).then_inc(var1, 1)

            def normalise_in(g):
                normalise(g, x_all, g * J, mv_in, rstd_in, rstd1, xn_in, xn1)

            def take_mod(g):
                nc.vector.tensor_copy(mod_now[:], mod[:, :, bass.ts(g, BG)]).then_inc(mod_taken, 1)

            def split_h1(g):
                att_count[0] = 0
                dve.wait_ge(h1_act, BG * (g + 1))
                att_signal(nc.vector.tensor_copy(h1_hi[:], h1[:]))
                att_wait(g)
                nc.vector.tensor_tensor(h1_lo[:], h1[:], h1_hi[:].bitcast(F32), ALU.subtract).then_inc(h1_split, 1)

            def clamp_a(g):
                dve.wait_ge(a_mm, g + 1)
                nc.vector.tensor_scalar(a_in[:], bank_b[:], bqka[:, 2:3], A_LEAST, ALU.add,
                                        ALU.max).then_inc(a_clamped, 1)

            def v_of(g):
                dve.wait_ge(v_mm, g + 1)
                nc.vector.tensor_tensor(v[:, :, 0:D], bank_a[:].rearrange("p (j d) -> p j d", j=J),
                                        bv[:].unsqueeze(1).to_broadcast([P, J, D]), ALU.add).then_inc(v_done, 1)

            def sum_logs(g):
                dve.wait_ge(a_logs, 2 * (g + 1))
                for b in range(BG):
                    back = slice(b * S + S - 1, b * S - 1 if b else None, -1)
                    nc.vector.tensor_tensor_scan(log_g[:, back], a_up[:, back], a_down[:, back], 0.0,
                                                 ALU.add, ALU.subtract).then_inc(log_g_done, 1)

            def decay_k(g):
                dve.wait_ge(decay_done, g + 1)
                dve.wait_ge(k_done, g + 1)
                nc.vector.tensor_tensor(wkT[:], kT[:], decay[:], ALU.mult).then_inc(wk_done, 1)

            def mask_scores(g):
                for b, ps in enumerate((bank_b, bank_c)):
                    dve.wait_ge(s_mm, BG * g + b + 1)
                    nc.vector.tensor_tensor(scores[:, b, :], ps[:, 0:SC], causal[:], ALU.mult).then_inc(s_masked, 1)

            def add_attention(g):
                if not isinstance(g, int) or g > 0:
                    dve.wait_ge(x2_kept, g)
                """x2 = x + num / (den + eps), ga being in num already; its mean and var + eps"""
                for b, ps in enumerate((bank_d, bank_a)):
                    dve.wait_ge(av_mm, BG * g + b + 1)
                    att_signal(nc.vector.tensor_scalar_add(
                        den[:, b * JB:(b + 1) * JB], ps[:].rearrange("p (j n) -> p j n", j=JB)[:, :, D], DEN_EPS))
                att_wait(g)
                att_signal(nc.vector.reciprocal(rden[:], den[:]))
                att_wait(g)
                first = att_count[0]
                for b, ps in enumerate((bank_d, bank_a)):
                    for j in range(JB):
                        t = b * JB + j
                        att_signal(nc.vector.scalar_tensor_tensor(
                            out=x2[:, t, :], in0=ps[:, j * S:j * S + D], scalar=rden[:, t:t + 1],
                            in1=x_all[:, g * J + t, :], op0=ALU.mult, op1=ALU.add))
                for j in range(J):
                    dve.wait_ge(att_step, ATT_STEPS * g + first + j + 1)
                    att_signal(nc.vector.bn_stats(stats[:, j, :], x2[:, j, :]))
                att_hold(g)
                for j in range(J):
                    att_signal(nc.vector.bn_aggr(mv[:, j, :], stats[:, j, :]))
                att_wait(g)
                nc.vector.tensor_scalar_add(var_eps[:], mv[:, :, 1], LN_EPS).then_inc(var2, 1)
                assert att_count[0] == ATT_STEPS, att_count

            def normalise_x2(g):
                normalise(g, x2, 0, mv, rstd, rstd2, xn, xn2)

            def split_h2(g):
                dve.wait_ge(h2_act, BG * (g + 1))
                nc.vector.tensor_copy(h2_hi[:], h2[:]).then_inc(h2_split, 1)
                dve.wait_ge(h2_split, 2 * g + 1)
                nc.vector.tensor_tensor(h2_lo[:], h2[:], h2_hi[:].bitcast(F32), ALU.subtract).then_inc(h2_split, 1)

            def route(g):
                route_count[0] = 0
                dve.wait_ge(logits_mm, g + 1)
                route_signal(nc.vector.tensor_tensor(logits[:], bank_c[:, 0:J * E].rearrange("p (j e) -> p j e", j=J),
                                                     bgate[:].unsqueeze(1).to_broadcast([P, J, E]), ALU.add))
                route_wait(g)
                one = logits[:].unsqueeze(3).to_broadcast([P, J, E, E])
                other = logits[:].unsqueeze(2).to_broadcast([P, J, E, E])
                route_signal(nc.vector.tensor_tensor(equal[:], other, one, ALU.is_equal))
                for j in range(J):
                    route_signal(nc.vector.max(top[:, j, :], logits[:, j, :]))
                route_wait(g)
                nc.vector.tensor_tensor(gap[:], top[:, :, 1], top[:, :, 0], ALU.subtract).then_inc(gap_done, 1)
                route_signal(nc.vector.tensor_tensor(
                    equal[:], equal[:], before[:].unsqueeze(1).to_broadcast([P, J, E, E]), ALU.mult))
                route_signal(nc.vector.tensor_tensor(larger[:], other, one, ALU.is_gt))
                route_wait(g)
                route_signal(nc.vector.tensor_tensor(larger[:], larger[:], equal[:], ALU.add))
                route_wait(g)
                dve.wait_ge(gap_exp, g + 1)
                nc.vector.tensor_reduce(rank[:], larger[:], AX.X, ALU.add).then_inc(rank_done, 1)
                route_signal(nc.vector.tensor_scalar_add(p_sum[:], p_gap[:], 1.0))
                route_wait(g)
                route_signal(nc.vector.reciprocal(share1[:], p_sum[:]))
                route_wait(g)
                route_signal(nc.vector.tensor_tensor(share2[:], p_gap[:], share1[:], ALU.mult))
                dve.wait_ge(rank_done, g + 1)
                nc.vector.scalar_tensor_tensor(
                    out=comb1[:], in0=rank[:], scalar=0.0, in1=share1[:].unsqueeze(2).to_broadcast([P, J, E]),
                    op0=ALU.is_equal, op1=ALU.mult).then_inc(comb1_done, 1)
                route_wait(g)
                route_signal(nc.vector.scalar_tensor_tensor(
                    out=comb2[:], in0=rank[:], scalar=1.0, in1=share2[:].unsqueeze(2).to_broadcast([P, J, E]),
                    op0=ALU.is_equal, op1=ALU.mult))
                route_wait(g)
                dve.wait_ge(comb1_done, g + 1)
                nc.vector.tensor_tensor(comb[:], comb1[:], comb2[:], ALU.add).then_inc(comb_done, 1)
                assert route_count[0] == ROUTE_STEPS, route_count

            def split_comb(g):
                nc.vector.tensor_copy(comb_hi[:], comb[:].rearrange("p j e -> p (j e)")).then_inc(halved, 1)
                dve.wait_ge(halved, 3 * g + 1)
                nc.vector.tensor_copy(comb_halves[:, 0::2, :],
                                      comb_hi[:].bitcast(F32).unsqueeze(1).to_broadcast([P, 2, J * E])).then_inc(halved, 1)
                nc.vector.tensor_tensor(comb_halves[:, 1::2, :],
                                        comb[:].rearrange("p j e -> p (j e)").unsqueeze(1).to_broadcast([P, 2, J * E]),
                                        comb_hi[:].bitcast(F32).unsqueeze(1).to_broadcast([P, 2, J * E]),
                                        ALU.subtract).then_inc(halved, 1)

            def copy_combT(g):
                dve.wait_ge(comb_T, g + 1)
                nc.vector.tensor_copy(combT[:], bank_c[:, 0:P]).then_inc(combT_done, 1)

            def add_expert(g, e):
                dve.wait_ge(y_mm, E * g + e + 1)
                y = y_ps[e % 2][:].rearrange("p (j d) -> p j d", j=J)
                if e == 0:
                    dve.wait_ge(comb_done, g + 1)
                    dve.wait_ge(acc_free, g + 1)
                if e == B2_AFTER + 1:
                    dve.wait_ge(acc_step, ACC_STEPS * g + acc_steps(B2_AFTER) + 1)
                for j in range(J):
                    weight = comb[:, j, e:e + 1]
                    if e == 0:
                        nc.vector.tensor_scalar(acc[:, j, :], y[:, j, :], weight, None, ALU.mult).then_inc(acc_step, 1)
                        continue
                    if e != B2_AFTER + 1:
                        dve.wait_ge(acc_step, ACC_STEPS * g + acc_steps(e - 1) - J + j + 1)
                    nc.vector.scalar_tensor_tensor(out=acc[:, j, :], in0=y[:, j, :], scalar=weight,
                                                   in1=acc[:, j, :], op0=ALU.mult,
                                                   op1=ALU.add).then_inc(acc_step, 1)

            def add_b2(g):
                dve.wait_ge(b2_mm, g + 1)
                dve.wait_ge(acc_step, ACC_STEPS * g + acc_steps(B2_AFTER))
                nc.vector.tensor_tensor(acc[:].rearrange("p j d -> p (j d)"), bank_c[:],
                                        acc[:].rearrange("p j d -> p (j d)"), ALU.add).then_inc(acc_step, 1)

            def experts(g, following, preparing):
                if following:
                    take_mod(g + 1)
                route(g)
                if following:
                    split_h1(g + 1)
                add_expert(g, 0)
                if following:
                    clamp_a(g + 1)
                add_expert(g, 1)
                if following:
                    v_of(g + 1)
                if preparing:
                    measure_in(g + 2)
                if following:
                    sum_logs(g + 1)
                if preparing:
                    normalise_in(g + 2)
                if following:
                    decay_k(g + 1)
                add_expert(g, 2)
                dve.wait_ge(comb_done, g + 1)
                split_comb(g)
                if following:
                    mask_scores(g + 1)
                add_expert(g, 3)
                if following:
                    add_attention(g + 1)
                add_expert(g, 4)
                if following:
                    normalise_x2(g + 1)
                copy_combT(g)
                add_expert(g, 5)
                add_b2(g)
                if following:
                    split_h2(g + 1)
                add_expert(g, 6)
                add_expert(g, 7)

            def finish_last():
                g = G - 1
                dve.wait_ge(x2_kept, G)
                dve.wait_ge(acc_free, G)
                dve.wait_ge(result, G - 1)
                for b in range(BG):
                    rows = slice(b * JB, (b + 1) * JB)
                    both = slice(g * J + b * JB, g * J + (b + 1) * JB)
                    dve.wait_ge(acc_step, ACC_STEPS * g + acc_steps(E - 1) - J + (b + 1) * JB)
                    nc.vector.tensor_tensor(scaled[:, rows, :], acc[:, rows, :],
                                            gates[:, g * BG + b, 1, :].unsqueeze(1).to_broadcast([P, JB, D]),
                                            ALU.mult).then_inc(last_step, 1)
                    dve.wait_ge(last_step, b + 1)
                    nc.vector.tensor_tensor(x_all[:, both, :], scaled[:, rows, :], x_all[:, both, :],
                                            ALU.add).then_inc(last_rows, 1)

            def split_w1_low(i):
                cols = slice(i * E * H // 4, (i + 1) * E * H // 4)
                nc.vector.tensor_tensor(w1_lo[:, cols], w1[:, cols], w1_hi[:, cols].bitcast(F32),
                                        ALU.subtract).then_inc(w1_split, 1)

            dve.wait_ge(in_x0, 16)
            measure_in(0)
            dve.wait_ge(c_exp_done, 1)
            after_once(nc.vector.tensor_scalar_add(c_den[:], c_exp[:], 1.0))
            after_once(nc.vector.reciprocal(c_rec[:], c_den[:]))
            nc.vector.tensor_tensor(c_silu[:], c_in[:], c_rec[:], ALU.mult).then_inc(silu_done, 1)
            normalise_in(0)
            dve.wait_ge(in_watt, 16)
            after_once(nc.vector.tensor_copy(watt_hi[:], watt[:, 0:3, :]))
            nc.vector.tensor_tensor(watt_lo[:], watt[:, 0:3, :], watt_hi[:].bitcast(F32),
                                    ALU.subtract).then_inc(watt_split, 1)
            dve.wait_ge(mod_mm, 1)
            mod_ps = z_ps[0][:, 0:4 * B].rearrange("p (m b) -> p m b", m=4)
            nc.vector.tensor_copy(mod[:, 0:3:2, :], mod_ps[:, 0:3:2, :]).then_inc(mod_ready, 1)
            nc.vector.tensor_scalar_add(mod[:, 1:4:2, :], mod_ps[:, 1:4:2, :], 1.0).then_inc(mod_ready, 1)
            dve.wait_ge(mod_ready, 2)
            take_mod(0)
            dve.wait_ge(gate_mm, 1)
            g_ps = y_ps[0][0:B, 0:2 * D]
            after_once(nc.vector.tensor_copy(g_raw[:], g_ps))
            nc.vector.tensor_scalar(g_sign[:], g_raw[:], 0.0, 2.0, ALU.is_ge, ALU.mult).then_inc(gate_step, 1)
            after_once(nc.vector.scalar_tensor_tensor(out=g_neg[:], in0=g_raw[:], scalar=-1.0, in1=g_raw[:],
                                                      op0=ALU.mult, op1=ALU.max))
            after_once(nc.vector.tensor_scalar_max(g_mag[:], g_neg[:], G_LEAST))
            dve.wait_ge(gate_step, 1)
            nc.vector.scalar_tensor_tensor(out=g_out[:], in0=g_sign[:], scalar=-1.0, in1=g_mag[:],
                                           op0=ALU.add, op1=ALU.mult).then_inc(g_ready, 1)
            split_h1(0)
            dve.wait_ge(in_x1, 16)
            measure_in(1)
            dve.wait_ge(in_bqka, 16)
            clamp_a(0)
            dve.wait_ge(in_bv, 16)
            dve.wait_ge(v_ones, 1)
            v_of(0)
            dve.wait_ge(in_w1, 16)
            after_once(nc.vector.tensor_copy(w1_hi[:], w1[:]))
            sum_logs(0)
            split_w1_low(0)
            decay_k(0)
            split_w1_low(1)
            split_w1_low(2)
            dve.wait_ge(pool_const, 6)
            mask_scores(0)
            normalise_in(1)
            add_attention(0)
            split_w1_low(3)
            normalise_x2(0)
            dve.wait_ge(in_b2, 16 * P // E)
            after_once(nc.vector.tensor_copy(b2_halves[:], b2d[:]))
            split_h2(0)
            nc.vector.tensor_tensor(b2_halves[P // 2:], b2d[P // 2:], b2_halves[P // 2:].bitcast(F32),
                                    ALU.subtract).then_inc(b2_split, 1)
            dve.wait_ge(in_bg, 16)
            dve.wait_ge(in_rest, 16)
            with dve.Fori(0, G - 2) as g:
                experts(g, True, True)
            experts(G - 2, True, False)
            experts(G - 1, False, False)
            finish_last()

        @block.tensor
        def _(pe):
            def mm(dst, lhsT, rhs, start=True, stop=True):
                return nc.tensor.matmul(dst, lhsT, rhs, start=start, stop=stop)

            def in_halves(dst, w_hi, w_lo, m_hi, m_lo):
                mm(dst, w_hi, m_hi, stop=False)
                mm(dst, w_hi, m_lo, start=False, stop=False)
                return mm(dst, w_lo, m_hi, start=False)

            def transpose_rows(g, rows, ready, ps, done):
                pe.wait_ge(ready, J * (g + 1))
                for j in range(J):
                    last = nc.tensor.transpose(ps[:, j * P:(j + 1) * P], rows[:, j, :], ident[:])
                last.then_inc(done, 1)

            def a_and_k(g):
                pe.wait_ge(h1_split, g + 1)
                in_halves(bank_b[:], watt_hi[:, 2, :], watt_lo[:, 2, :], h1_hi[:], h1_lo[:]).then_inc(a_mm, 1)
                in_halves(bank_c[:], watt_hi[:, 1, :], watt_lo[:, 1, :], h1_hi[:], h1_lo[:]).then_inc(k_mm, 1)

            def v_of(g):
                for j in range(J):
                    last = mm(bank_a[:, j * D:(j + 1) * D], h1[:, j * P:(j + 1) * P], watt[:, 3, :])
                last.then_inc(v_mm, 1)

            def q_of(g):
                in_halves(bank_d[:], watt_hi[:, 0, :], watt_lo[:, 0, :], h1_hi[:], h1_lo[:]).then_inc(q_mm, 1)

            def scores_of(g):
                pe.wait_ge(wk_done, g + 1)
                pe.wait_ge(q_done, g + 1)
                for b, ps in enumerate((bank_b, bank_c)):
                    t0 = b * S
                    mm(ps[:, 0:S], wkT[:, t0:t0 + P], qT[:, t0:t0 + S])
                    mm(ps[:, S:SC], wkT[:, t0 + P:t0 + S], qT[:, t0 + P:t0 + S]).then_inc(s_mm, 1)

            def values_of(g):
                pe.wait_ge(v_gated, g + 1)
                for b, ps in enumerate((bank_d, bank_a)):
                    pe.wait_ge(s_masked, BG * g + b + 1)
                    mm(ps[:, 0:D + 1], scores[:, b, 0:P], v[:, b * JB, 0:D + 1])
                    mm(ps[:, S:S + D + 1], scores[:, b, P:S], v[:, b * JB, 0:D + 1], stop=False)
                    mm(ps[:, S:S + D + 1], scores[:, b, S:SC], v[:, b * JB + 1, 0:D + 1],
                       start=False).then_inc(av_mm, 1)

            def logits_of(g):
                pe.wait_ge(h2_act, BG * (g + 1))
                if not isinstance(g, int) or g > 0:
                    pe.wait_ge(acc_step, ACC_STEPS * (g - 1) + acc_steps(B2_AFTER) + 1)
                for j in range(J):
                    last = mm(bank_c[:, j * E:(j + 1) * E], h2[:, j * P:(j + 1) * P], wg[:])
                last.then_inc(logits_mm, 1)

            def transpose_comb(g):
                pe.wait_ge(halved, 3 * (g + 1))
                nc.tensor.transpose(bank_c[:, 0:P], comb_halves[:].rearrange("p h n -> p (h n)"),
                                    ident[:]).then_inc(comb_T, 1)

            def b2_of(g):
                pe.wait_ge(combT_done, g + 1)
                mm(bank_c[:], combT[:], b2_halves[:].rearrange("k j d -> k (j d)")).then_inc(b2_mm, 1)

            def hidden(g, e):
                for hb in range(HB):
                    if e > 0:
                        pe.wait_ge(relu_done, HB * (E * g + e - 1) + hb + 1)
                    w = slice((HB * e + hb) * P, (HB * e + hb + 1) * P)
                    in_halves(z_ps[hb][:], w1_hi[:, w], w1_lo[:, w], h2_hi[:], h2_lo[:]).then_inc(z_mm, 1)

            def expert_out(g, e):
                pe.wait_ge(relu_done, HB * (E * g + e) + HB)
                if e >= 2:
                    pe.wait_ge(acc_step, ACC_STEPS * g + acc_steps(e - 2))
                else:
                    pe.wait_ge(gap_done, g + 1)
                for j in range(J):
                    for hb in range(HB):
                        last = mm(y_ps[e % 2][:, j * D:(j + 1) * D], relu[:, e % 2, hb, j * P:(j + 1) * P],
                                  w2[:, e, hb, :], start=hb == 0, stop=hb == HB - 1)
                last.then_inc(y_mm, 1)

            def experts(g, following):
                hidden(g, 0)
                if following:
                    transpose_rows(g + 1, xn_in, xn1, bank_a, xn1_T)
                hidden(g, 1)
                expert_out(g, 0)
                hidden(g, 2)
                if following:
                    a_and_k(g + 1)
                expert_out(g, 1)
                hidden(g, 3)
                if following:
                    v_of(g + 1)
                    q_of(g + 1)
                expert_out(g, 2)
                hidden(g, 4)
                expert_out(g, 3)
                if following:
                    scores_of(g + 1)
                hidden(g, 5)
                if following:
                    values_of(g + 1)
                expert_out(g, 4)
                hidden(g, 6)
                transpose_comb(g)
                expert_out(g, 5)
                hidden(g, 7)
                b2_of(g)
                if following:
                    transpose_rows(g + 1, xn, xn2, bank_b, xn2_T)
                expert_out(g, 6)
                expert_out(g, 7)
                if following:
                    logits_of(g + 1)
                    pe.wait_ge(h2_split, 2 * (g + 2))

            pe.wait_ge(in_wmod, 16)
            pe.wait_ge(silu_done, 1)
            for i, chunk in enumerate((0, 1, 3, 4)):
                last = mm(z_ps[0][:, i * B:(i + 1) * B], wm[:, chunk, :], c_silu[:])
            last.then_inc(mod_mm, 1)
            for i, chunk in enumerate((2, 5)):
                last = mm(y_ps[0][0:B, i * D:(i + 1) * D], c_silu[:], wm[:, chunk, :])
            last.then_inc(gate_mm, 1)

            pe.wait_ge(pool_const, 6)
            transpose_rows(0, xn_in, xn1, bank_a, xn1_T)
            pe.wait_ge(watt_split, 1)
            a_and_k(0)
            v_of(0)
            q_of(0)
            scores_of(0)
            values_of(0)
            transpose_rows(0, xn, xn2, bank_b, xn2_T)
            pe.wait_ge(in_wg, 16)
            logits_of(0)
            pe.wait_ge(h2_split, 2)
            pe.wait_ge(w1_split, 4)
            pe.wait_ge(in_w2, 16)
            pe.wait_ge(b2_split, 1)
            with pe.Fori(0, G - 1) as g:
                experts(g, True)
            experts(G - 1, False)


def kernel(**inputs):
    import numpy as np
    import concourse.bacc as bacc
    from concourse.bass_utils import run_bass_kernel_spmd

    def a(name):
        return np.asarray(inputs["L0_" + name])

    arrays = {
        "x": a("attn_x_seq").reshape(T, D),
        "w_att": np.concatenate([a(f"attn_W_{m}").T for m in "qkav"], axis=1),
        "b_qka": np.stack([a(f"attn_b_{m}") for m in "qka"], axis=1),
        "b_v": a("attn_b_v"),
        "w1t": a("ffn_W1").transpose(2, 0, 1).reshape(D, E * H),
        "b1t": a("ffn_b1").reshape(E * HB, P).T,
        "w2t": a("ffn_W2").reshape(E, D, HB, P).transpose(3, 0, 2, 1).reshape(P, E * HB * D),
        "b2": a("ffn_b2"),
        "wgt": a("ffn_Wg").T,
        "bg": a("ffn_bg"),
        "ct": a("c").T,
        "wmod": a("wmod"),
    }
    arrays = {name: np.ascontiguousarray(value) for name, value in arrays.items()}
    nc = bacc.Bacc("TRN2", target_bir_lowering=False, num_devices=1)
    args = {name: nc.dram_tensor(f"{name}_dram", value.shape, F32, kind="ExternalInput").ap()
            for name, value in arrays.items()}
    out = nc.dram_tensor("out_dram", (T, D), F32, kind="ExternalOutput").ap()
    gate_rows = nc.dram_tensor("gate_rows", (B, 2 * D), F32, kind="Internal").ap()
    adaln_block(nc, out=out, gate_rows=gate_rows, **args)
    got = run_bass_kernel_spmd(nc, [{f"{name}_dram": value for name, value in arrays.items()}], core_ids=[0])
    return got.results[0]["out_dram"].reshape(B, S, D)
```

```python
from contextlib import ExitStack

import concourse.bass as bass
from concourse import mybir

F32 = mybir.dt.float32
F32R = mybir.dt.float32r
ALU = mybir.AluOpType
ACT = mybir.ActivationFunctionType
AX = mybir.AxisListType

P = 128
B, S, D = 16, 256, 128
E, H = 8, 256
HB = H // P
T = B * S
TG = 4 * P
G = T // TG
J = TG // P
BG = TG // S
JB = S // P
VW = D + 4
SEQUENCES = [slice(b * S, (b + 1) * S) for b in range(BG)]
WARM_START, WARM_SPLIT, WARM_DECAY, WARM_MASK, WARM_NORM, WARM_H2 = 15, 2, 4, 4, 32, 4
COLUMNS = B + 3 + E * HB + E
SC = S + P
LN_EPS = 1e-5
DEN_EPS = 1e-6
LOG_EPS = 1e-6
A_LEAST = -69.0
G_LEAST = 0.25


def adaln_block(nc, x, w_att, column_inputs, row_inputs, w1t, w2t, b2, wmod, out, gate_rows):
    ctx = ExitStack()
    with ctx:
        def sb(name, shape, dt=F32):
            return ctx.enter_context(nc.sbuf_tensor(name, shape, dt))

        def sem(name):
            return ctx.enter_context(nc.semaphore(name))

        x_all = sb("x_all", [P, G * J, D])
        gates = sb("gates", [P, B, 2, D])
        mod = sb("mod", [P, 4, B])
        watt = sb("watt", [P, 4, D])
        watt_hi = sb("watt_hi", [P, 3, D], F32R)
        watt_lo = sb("watt_lo", [P, 3, D], F32R)
        w1 = sb("w1", [P, E * H])
        w1_hi = sb("w1_hi", [P, E * H], F32R)
        w1_lo = sb("w1_lo", [P, E * H], F32R)
        w2 = sb("w2", [P, E, HB, D])
        column_data = sb("column_data", [P, COLUMNS])
        row_data = sb("row_data", [P, D + E])
        c_in, bqka, b1, wg = (column_data[:, i:j] for i, j in ((0, B), (B, B + 3), (B + 3, B + 3 + E * HB),
                                                                (B + 3 + E * HB, COLUMNS)))
        bv, bgate = row_data[:, 0:D], row_data[:, D:D + E]
        b2d = sb("b2d", [P, J, D])
        b2_halves = sb("b2_halves", [P, J, D], F32R)
        ident = sb("ident", [P, P])
        causal = sb("causal", [P, SC])
        before = sb("before", [P, E, E])
        half_power = sb("half_power", [P, J])
        carrier = sb("carrier", [P, 1])
        log_bias = sb("log_bias", [P, 1])
        c_exp = sb("c_exp", [P, B])
        c_den = sb("c_den", [P, B])
        c_rec = sb("c_rec", [P, B])
        c_silu = sb("c_silu", [P, B])
        wm = sb("wm", [P, 6, D])
        g_raw = sb("g_raw", [B, 2 * D])
        g_abs = sb("g_abs", [B, 2 * D])
        g_mag = sb("g_mag", [B, 2 * D])
        g_sign = sb("g_sign", [B, 2 * D])
        g_out = sb("g_out", [B, 2 * D])
        stats = sb("stats", [P, J, 6])
        mv = sb("mv", [P, J, 2])
        var_eps = sb("var_eps", [P, J])
        rstd = sb("rstd", [P, J])
        xn = sb("xn", [P, J, D])
        stats_in = sb("stats_in", [P, J, 6])
        mv_in = sb("mv_in", [P, J, 2])
        var_in = sb("var_in", [P, J])
        rstd_in = sb("rstd_in", [P, J])
        xn_in = sb("xn_in", [P, J, D])
        x2 = sb("x2", [P, J, D])
        mod_now = sb("mod_now", [P, 4, BG])
        h1 = sb("h1", [P, TG])
        h1_hi = sb("h1_hi", [P, TG], F32R)
        h1_lo = sb("h1_lo", [P, TG], F32R)
        h2 = sb("h2", [P, TG])
        h2_hi = sb("h2_hi", [P, TG], F32R)
        h2_lo = sb("h2_lo", [P, TG], F32R)
        a_in = sb("a_in", [P, TG])
        a_exp = sb("a_exp", [P, TG])
        a_up = sb("a_up", [P, TG])
        a_down = sb("a_down", [P, TG])
        log_g = sb("log_g", [P, TG])
        decay = sb("decay", [P, TG])
        qT = sb("qT", [P, TG])
        kT = sb("kT", [P, TG])
        wkT = sb("wkT", [P, TG])
        v = sb("v", [P, J, VW])
        scores = sb("scores", [P, BG, SC])
        den = sb("den", [P, J])
        rden = sb("rden", [P, J])
        logits = sb("logits", [P, J, E])
        top = sb("top", [P, J, 8])
        gap = sb("gap", [P, J])
        p_gap = sb("p_gap", [P, J])
        p_sum = sb("p_sum", [P, J])
        share1 = sb("share1", [P, J])
        share2 = sb("share2", [P, J])
        larger = sb("larger", [P, J, E, E])
        equal = sb("equal", [P, J, E, E])
        rank = sb("rank", [P, J, E])
        comb1 = sb("comb1", [P, J, E])
        comb2 = sb("comb2", [P, J, E])
        comb = sb("comb", [P, J, E])
        comb_hi = sb("comb_hi", [P, J, E], F32R)
        comb_halves = sb("comb_halves", [P, 2, J, 2, E])
        combT = sb("combT", [P, P], F32R)
        relu = sb("relu", [P, 2, HB, TG])
        acc = sb("acc", [P, J, D])
        scaled = sb("scaled", [P, J, D])
        def bank(name):
            return ctx.enter_context(nc.psum_tensor(name, [P, 512], F32))

        z_ps = [bank("z0"), bank("z1")]
        y_ps = [bank("y0"), bank("y1")]
        bank_a, bank_b, bank_c, bank_d = bank("bank_a"), bank("bank_b"), bank("bank_c"), bank("bank_d")

        def halves_of(ps):
            return [ps[:, b * S:(b + 1) * S] for b in range(BG)]

        FIRST_XN1 = [bank_a[:, 0:S], bank_c[:, 0:S]]
        FIRST_A = [bank_b[:, 0:S], y_ps[1][:, 0:S]]
        FIRST_XN2 = [bank_b[:, 0:S], y_ps[1][:, 0:S]]

        LAST_Y = [y_ps[1], bank_a]

        def needed(g, b, apart):
            return BG * g + (b + 1 if apart else BG)

        in_columns, in_rows, in_wmod_a, in_wmod_b, in_x0, in_watt, in_b2, in_w1, in_w2, in_rest = (
            sem(n) for n in ("in_columns", "in_rows", "in_wmod_a", "in_wmod_b", "in_x0", "in_watt", "in_b2",
                             "in_w1", "in_w2", "in_rest"))
        ident_made, pool_step, pool_const, b2_zero, v_ones = (
            sem(n) for n in ("ident_made", "pool_step", "pool_const", "b2_zero", "v_ones"))
        c_exp_done, silu_done, mod_mm, gate_mm, mod_ready, g_taken, gate_step, g_ready, g_stored, g_loaded = (
            sem(n) for n in ("c_exp_done", "silu_done", "mod_mm", "gate_mm", "mod_ready", "g_taken", "gate_step", "g_ready",
                             "g_stored", "g_loaded"))
        g0_loaded = sem("g0_loaded")
        watt_split, w1_high, w1_split, once_step = sem("watt_split"), sem("w1_high"), sem("w1_split"), sem("once_step")
        var1, rstd1, xn1, xn1_T, h1_act, h1_split = (
            sem(n) for n in ("var1", "rstd1", "xn1", "xn1_T", "h1_act", "h1_split"))
        a_mm, k_mm, q_mm, v_mm = sem("a_mm"), sem("k_mm"), sem("q_mm"), sem("v_mm")
        a_clamped, a_exp_done, a_logs, log_g_done, decay_done = (
            sem(n) for n in ("a_clamped", "a_exp_done", "a_logs", "log_g_done", "decay_done"))
        k_done, q_done, v_done, wk_done = sem("k_done"), sem("q_done"), sem("v_done"), sem("wk_done")
        s_mm, s_masked, av_mm = sem("s_mm"), sem("s_masked"), sem("av_mm")
        var2, rstd2, xn2, xn2_T, h2_act, h2_split = (
            sem(n) for n in ("var2", "rstd2", "xn2", "xn2_T", "h2_act", "h2_split"))
        logits_mm, gap_done, gap_exp, comb_done, comb_T, combT_done, b2_mm = (
            sem(n) for n in ("logits_mm", "gap_done", "gap_exp", "comb_done", "comb_T", "combT_done", "b2_mm"))
        z_mm, relu_done, y_mm, acc_step, acc_free, result, stored = (
            sem(n) for n in ("z_mm", "relu_done", "y_mm", "acc_step", "acc_free", "result", "stored"))
        mod_taken, mod_late, v_gated, x2_kept, norm_step = (
            sem(n) for n in ("mod_taken", "mod_late", "v_gated", "x2_kept", "norm_step"))
        in_x1, halved, b2_high, b2_split, last_rows, last_step, y_last = (
            sem(n) for n in ("in_x1", "halved", "b2_high", "b2_split", "last_rows", "last_step", "y_last"))
        att_step, route_step, rank_done, comb1_done = (
            sem(n) for n in ("att_step", "route_step", "rank_done", "comb1_done"))

        B2_AFTER = 5
        ACC_STEPS = E * J + 1

        def acc_steps(e):
            return (e + 1) * J + (e > B2_AFTER)

        x_dram = x.rearrange("(n p) d -> p n d", p=P)
        out_dram = out.rearrange("(n p) d -> p n d", p=P)

        block = ctx.enter_context(nc.Block())

        @block.sync
        def _(sp):
            sp.dma_start(x_all[:, 0:J, :], x_dram[:, 0:J, :]).then_inc(in_x0, 16)
            sp.dma_start(watt[:].rearrange("p m n -> p (m n)"), w_att).then_inc(in_watt, 16)
            sp.dma_start(x_all[:, J:2 * J, :], x_dram[:, J:2 * J, :]).then_inc(in_x1, 16)
            sp.dma_start(w1[:], w1t).then_inc(in_w1, 16)
            sp.dma_start(w2[:].rearrange("p e h n -> p (e h n)"), w2t).then_inc(in_w2, 16)
            sp.wait_ge(b2_zero, 1)
            for j in range(J):
                for row in (2 * E * j, P // 2 + 2 * E * j):
                    sp.dma_start(b2d[row:row + 2 * E, j, :], b2).then_inc(in_b2, 16)
            sp.wait_ge(g_ready, 1)
            sp.dma_start(gate_rows, g_out[:]).then_inc(g_stored, 16)
            sp.wait_ge(g_stored, 16)
            for some, loaded in ((slice(0, BG), g0_loaded), (slice(BG, B), g_loaded)):
                sp.dma_start(gates[:, some].rearrange("p b m n -> p (b m n)"),
                             gate_rows[some, :].rearrange("b n -> (b n)").partition_broadcast(P)).then_inc(loaded, 16)
                if some.start == 0:
                    sp.dma_start(x_all[:, 2 * J:G * J, :], x_dram[:, 2 * J:G * J, :]).then_inc(in_rest, 16)
            with sp.Fori(0, G - 1) as g:
                sp.wait_ge(result, g + 1)
                sp.dma_start(out_dram[:, bass.ts(g, J), :], x_all[:, bass.ts(g, J), :]).then_inc(stored, 16)
            for b in range(BG):
                rows = slice((G - 1) * J + b * JB, (G - 1) * J + (b + 1) * JB)
                sp.wait_ge(last_rows, b + 1)
                sp.dma_start(out_dram[:, rows, :], x_all[:, rows, :]).then_inc(stored, 16)
            sp.wait_ge(stored, 16 * (G - 1 + BG))

        @block.gpsimd
        def _(pool):
            nc.gpsimd.memset(ident[:], 1.0).then_inc(pool_step, 1)
            pool.wait_ge(pool_step, 1)
            nc.gpsimd.affine_select(out=ident[:], in_=ident[:], compare_op=ALU.is_equal, fill=0.0, base=0,
                                    pattern=[[1, P]], channel_multiplier=-1).then_inc(ident_made, 1)
            nc.gpsimd.memset(causal[:], 1.0).then_inc(pool_step, 1)
            nc.gpsimd.memset(before[:], 1.0).then_inc(pool_step, 1)
            nc.gpsimd.memset(half_power[:], -0.5).then_inc(pool_const, 1)
            nc.gpsimd.memset(log_bias[:], 1.0 + LOG_EPS).then_inc(pool_const, 1)
            nc.gpsimd.memset(v[:], 1.0).then_inc(v_ones, 1)
            nc.gpsimd.memset(scaled[:], 0.0).then_inc(acc_free, 1)
            nc.gpsimd.memset(b2d[:], 0.0).then_inc(b2_zero, 1)
            pool.wait_ge(pool_step, 3)
            for first in (0, S):
                nc.gpsimd.affine_select(out=causal[:, first:first + P], in_=causal[:, first:first + P],
                                        compare_op=ALU.is_ge, fill=0.0, base=0,
                                        pattern=[[1, P]], channel_multiplier=-1).then_inc(pool_const, 1)
            nc.gpsimd.affine_select(out=before[:], in_=before[:], compare_op=ALU.is_gt, fill=0.0, base=0,
                                    pattern=[[1, E], [-1, E]], channel_multiplier=0).then_inc(pool_const, 1)

            def rstd_of(g, var, var_ready, parts, power, rstd_done):
                for i in range(parts):
                    tiles = slice(i * J // parts, (i + 1) * J // parts)
                    pool.wait_ge(var_ready, parts * g + i + 1)
                    nc.gpsimd.tensor_tensor(power[:, tiles], var[:, tiles], half_power[:, tiles],
                                            ALU.pow).then_inc(rstd_done, 1)

            def gate_of(g, which):
                return gates[:, bass.ts(g, BG), which, :].unsqueeze(2).to_broadcast([P, BG, JB, D])

            def gate_v(g):
                for b in range(BG):
                    pool.wait_ge(v_done, BG * g + b + 1)
                    rows = v[:, b * JB:(b + 1) * JB, 0:D]
                    nc.gpsimd.tensor_tensor(rows, rows, gates[:, g * BG + b, 0, :].unsqueeze(1).to_broadcast([P, JB, D]),
                                            ALU.mult).then_inc(v_gated, 1)

            def finish(g):
                pool.wait_ge(x2_kept, g + 1)
                pool.wait_ge(acc_step, ACC_STEPS * (g + 1))
                nc.gpsimd.tensor_tensor(scaled[:].rearrange("p (b j) d -> p b j d", b=BG),
                                        acc[:].rearrange("p (b j) d -> p b j d", b=BG), gate_of(g, 1),
                                        ALU.mult).then_inc(acc_free, 1)
                pool.wait_ge(acc_free, g + 2)
                nc.gpsimd.tensor_tensor(x_all[:, bass.ts(g, J), :], scaled[:], x_all[:, bass.ts(g, J), :],
                                        ALU.add).then_inc(result, 1)
                pool.wait_ge(result, g + 1)

            def experts(g, following, preparing):
                if following:
                    gate_v(g + 1)
                if preparing:
                    rstd_of(g + 2, var_in, var1, 1, rstd_in, rstd1)
                if following:
                    rstd_of(g + 1, var_eps, var2, BG, rstd, rstd2)
                if following:
                    finish(g)

            def low_of_w1(i):
                cols = slice(i * E * H // 4, (i + 1) * E * H // 4)
                nc.gpsimd.tensor_tensor(w1_lo[:, cols], w1[:, cols], w1_hi[:, cols].bitcast(F32),
                                        ALU.subtract).then_inc(w1_split, 1)

            pool.wait_ge(pool_const, 5)
            rstd_of(0, var_in, var1, 1, rstd_in, rstd1)
            pool.wait_ge(g0_loaded, 16)
            gate_v(0)
            pool.wait_ge(w1_high, 1)
            low_of_w1(0)
            rstd_of(1, var_in, var1, 1, rstd_in, rstd1)
            low_of_w1(1)
            rstd_of(0, var_eps, var2, BG, rstd, rstd2)
            low_of_w1(2)
            low_of_w1(3)
            pool.wait_ge(in_b2, 16 * 2 * J)
            nc.gpsimd.tensor_copy(b2_halves[:], b2d[:]).then_inc(b2_high, 1)
            pool.wait_ge(b2_high, 1)
            nc.gpsimd.tensor_tensor(b2_halves[P // 2:], b2d[P // 2:], b2_halves[P // 2:].bitcast(F32),
                                    ALU.subtract).then_inc(b2_split, 1)
            pool.wait_ge(b2_split, 1)
            pool.wait_ge(g_loaded, 16)
            with pool.Fori(0, G - 2) as g:
                experts(g, True, True)
            experts(G - 2, True, False)

        @block.scalar
        def _(act):
            act.dma_start(column_data[:], column_inputs).then_inc(in_columns, 16)
            act.dma_start(wm[:, 0:2, :].rearrange("p m n -> p (m n)"), wmod[:, 0:2 * D]).then_inc(in_wmod_a, 16)
            nc.scalar.preload_act_table_set("natural_log_exp_and_others")
            act.dma_start(wm[:, 2:6, :].rearrange("p m n -> p (m n)"), wmod[:, 2 * D:6 * D]).then_inc(in_wmod_b, 16)
            act.dma_start(row_data[:], row_inputs.partition_broadcast(P)).then_inc(in_rows, 16)
            act.wait_ge(in_columns, 16)
            nc.scalar.activation(c_exp[:], c_in, ACT.Exp, scale=-1.0).then_inc(c_exp_done, 1)

            def modulate(g, dst, ready, places, apart, shift, done):
                for b in range(BG):
                    act.wait_ge(ready, needed(g, b, apart))
                    nc.scalar.activation(dst[:, b * S:(b + 1) * S], places[b], ACT.Identity,
                                         scale=mod_now[:, shift + 1, b:b + 1],
                                         bias=mod_now[:, shift, b:b + 1]).then_inc(done, 1)

            def h1_of(g, places, apart=False):
                act.wait_ge(mod_taken, g + 1)
                modulate(g, h1, xn1_T, places, apart, 0, h1_act)

            def a_of(g):
                for b, cols in enumerate(SEQUENCES):
                    act.wait_ge(a_clamped, BG * g + b + 1)
                    nc.scalar.activation(a_exp[:, cols], a_in[:, cols], ACT.Exp, scale=-1.0).then_inc(a_exp_done, 1)
                for b, cols in enumerate(SEQUENCES):
                    act.wait_ge(a_exp_done, BG * g + b + 1)
                    nc.scalar.activation(a_up[:, cols], a_exp[:, cols], ACT.Ln, scale=LOG_EPS,
                                         bias=log_bias[:]).then_inc(a_logs, 1)
                    nc.scalar.activation(a_down[:, cols], a_exp[:, cols], ACT.Ln, scale=1.0, bias=1.0).then_inc(a_logs, 1)

            def k_of(g):
                act.wait_ge(k_mm, g + 1)
                nc.scalar.activation(kT[:], bank_c[:], ACT.Relu, bias=bqka[:, 1:2]).then_inc(k_done, 1)

            def q_of(g):
                act.wait_ge(q_mm, g + 1)
                for cols in SEQUENCES:
                    nc.scalar.activation(qT[:, cols], bank_d[:, cols], ACT.Relu, bias=bqka[:, 0:1]).then_inc(q_done, 1)

            def decay_of(g):
                for b, cols in enumerate(SEQUENCES):
                    act.wait_ge(log_g_done, BG * g + b + 1)
                    nc.scalar.activation(decay[:, cols], log_g[:, cols], ACT.Exp).then_inc(decay_done, 1)

            def h2_of(g, places, apart=False):
                modulate(g, h2, xn2_T, places, apart, 2, h2_act)
                nc.scalar.copy(x_all[:, bass.ts(g, J), :], x2[:]).then_inc(x2_kept, 1)

            def gap_of(g):
                act.wait_ge(gap_done, g + 1)
                nc.scalar.activation(p_gap[:], gap[:], ACT.Exp).then_inc(gap_exp, 1)

            def relu_of(g, e):
                for hb in range(HB):
                    act.wait_ge(z_mm, HB * (E * g + e) + hb + 1)
                    nc.scalar.activation(relu[:, e % 2, hb, :], z_ps[hb][:], ACT.Relu,
                                         bias=b1[:, HB * e + hb:HB * e + hb + 1]).then_inc(relu_done, 1)

            def experts(g, following):
                for e in range(E):
                    relu_of(g, e)
                    if e == 0:
                        gap_of(g)
                        if following:
                            h1_of(g + 1, halves_of(bank_a))
                    if following and e == 2:
                        a_of(g + 1)
                        k_of(g + 1)
                    if following and e == 3:
                        q_of(g + 1)
                        decay_of(g + 1)
                    if following and e == E - 1:
                        h2_of(g + 1, halves_of(bank_b))

            act.wait_ge(pool_const, 5)
            h1_of(0, FIRST_XN1, True)
            act.wait_ge(gate_mm, 1)
            nc.scalar.copy(g_raw[:], y_ps[0][0:B, 0:2 * D]).then_inc(g_taken, 1)
            nc.scalar.activation(g_abs[:], y_ps[0][0:B, 0:2 * D], ACT.Abs).then_inc(g_taken, 1)
            a_of(0)
            decay_of(0)
            act.wait_ge(in_w1, 16)
            nc.scalar.copy(w1_hi[:], w1[:]).then_inc(w1_high, 1)
            act.wait_ge(mod_late, 1)
            h2_of(0, FIRST_XN2, True)
            with act.Fori(0, G - 1) as g:
                experts(g, True)
            experts(G - 1, False)

        ATT_STEPS = 3 * J + 3 * BG
        NORM_STEPS = 2 * J
        ROUTE_STEPS = J + 9

        @block.vector
        def _(dve):
            once = [0]

            def after_once(instruction):
                once[0] += 1
                instruction.then_inc(once_step, 1)
                dve.wait_ge(once_step, once[0])

            att_count, route_count = [0], [0]

            def att_signal(instruction):
                att_count[0] += 1
                instruction.then_inc(att_step, 1)

            def att_wait(g):
                dve.wait_ge(att_step, ATT_STEPS * g + att_count[0])

            def att_hold(g):
                att_wait(g)
                nc.vector.memset(carrier[:], 0.0)

            def route_signal(instruction):
                route_count[0] += 1
                instruction.then_inc(route_step, 1)

            def route_wait(g):
                dve.wait_ge(route_step, ROUTE_STEPS * g + route_count[0])

            def normalise(g, rows, at, mean_var, power, rstd_ready, parts, dst, done):
                for j in range(J):
                    if j % (J // parts) == 0:
                        dve.wait_ge(rstd_ready, parts * g + j * parts // J + 1)
                    nc.vector.tensor_scalar(dst[:, j, :], rows[:, at + j, :], mean_var[:, j, 0:1], power[:, j:j + 1],
                                            ALU.subtract, ALU.mult).then_inc(done, 1)

            def measure_in(g):
                stats_of_in(g, range(J))
                close_measure_in(g)

            def stats_of_in(g, tiles):
                for j in tiles:
                    nc.vector.bn_stats(stats_in[:, j, :], x_all[:, g * J + j, :]).then_inc(norm_step, 1)

            def close_measure_in(g):
                dve.wait_ge(norm_step, NORM_STEPS * g + J)
                nc.vector.memset(carrier[:], 0.0)
                for j in range(J):
                    nc.vector.bn_aggr(mv_in[:, j, :], stats_in[:, j, :]).then_inc(norm_step, 1)
                dve.wait_ge(norm_step, NORM_STEPS * (g + 1))
                nc.vector.tensor_scalar_add(var_in[:], mv_in[:, :, 1], LN_EPS).then_inc(var1, 1)

            def normalise_in(g):
                normalise(g, x_all, g * J, mv_in, rstd_in, rstd1, 1, xn_in, xn1)

            def take_mod(g):
                nc.vector.tensor_copy(mod_now[:], mod[:, :, bass.ts(g, BG)]).then_inc(mod_taken, 1)

            def split_h1(g):
                att_count[0] = 0
                for b, cols in enumerate(SEQUENCES):
                    dve.wait_ge(h1_act, BG * g + b + 1)
                    att_signal(nc.vector.tensor_copy(h1_hi[:, cols], h1[:, cols]))
                    att_wait(g)
                    nc.vector.tensor_tensor(h1_lo[:, cols], h1[:, cols], h1_hi[:, cols].bitcast(F32),
                                            ALU.subtract).then_inc(h1_split, 1)

            def clamp_a(g, places, apart=False):
                for b, cols in enumerate(SEQUENCES):
                    dve.wait_ge(a_mm, needed(g, b, apart))
                    nc.vector.tensor_scalar(a_in[:, cols], places[b], bqka[:, 2:3], A_LEAST, ALU.add,
                                            ALU.max).then_inc(a_clamped, 1)

            def v_of(g):
                dve.wait_ge(v_mm, g + 1)
                for b in range(BG):
                    rows = slice(b * JB, (b + 1) * JB)
                    nc.vector.tensor_tensor(v[:, rows, 0:D], bank_a[:].rearrange("p (j d) -> p j d", j=J)[:, rows, :],
                                            bv.unsqueeze(1).to_broadcast([P, JB, D]), ALU.add).then_inc(v_done, 1)

            def sum_logs(g, b):
                dve.wait_ge(a_logs, 2 * (BG * g + b + 1))
                back = slice(b * S + S - 1, b * S - 1 if b else None, -1)
                nc.vector.tensor_tensor_scan(log_g[:, back], a_up[:, back], a_down[:, back], 0.0,
                                             ALU.add, ALU.subtract).then_inc(log_g_done, 1)

            def decay_k(g):
                dve.wait_ge(k_done, g + 1)
                for b, cols in enumerate(SEQUENCES):
                    dve.wait_ge(decay_done, BG * g + b + 1)
                    nc.vector.tensor_tensor(wkT[:, cols], kT[:, cols], decay[:, cols], ALU.mult).then_inc(wk_done, 1)

            def mask_scores(g):
                for b, ps in enumerate((bank_b, bank_c)):
                    dve.wait_ge(s_mm, BG * g + b + 1)
                    nc.vector.tensor_tensor(scores[:, b, :], ps[:, 0:SC], causal[:], ALU.mult).then_inc(s_masked, 1)

            def add_attention(g):
                if not isinstance(g, int) or g > 0:
                    dve.wait_ge(x2_kept, g)
                """x2 = x + num / (den + eps), ga being in num already; its mean and var + eps"""
                x2_step = []
                for b, ps in enumerate((bank_d, bank_a)):
                    tiles = slice(b * JB, (b + 1) * JB)
                    dve.wait_ge(av_mm, BG * g + b + 1)
                    att_signal(nc.vector.tensor_scalar_add(
                        den[:, tiles], ps[:].rearrange("p (j n) -> p j n", j=JB)[:, :, D], DEN_EPS))
                    att_wait(g)
                    att_signal(nc.vector.reciprocal(rden[:, tiles], den[:, tiles]))
                    att_wait(g)
                    for j in range(JB):
                        t = b * JB + j
                        att_signal(nc.vector.scalar_tensor_tensor(
                            out=x2[:, t, :], in0=ps[:, j * S:j * S + D], scalar=rden[:, t:t + 1],
                            in1=x_all[:, g * J + t, :], op0=ALU.mult, op1=ALU.add))
                        x2_step.append(att_count[0])
                for b in range(BG):
                    tiles = slice(b * JB, (b + 1) * JB)
                    for j in range(b * JB, (b + 1) * JB):
                        dve.wait_ge(att_step, ATT_STEPS * g + x2_step[j])
                        att_signal(nc.vector.bn_stats(stats[:, j, :], x2[:, j, :]))
                    att_hold(g)
                    for j in range(b * JB, (b + 1) * JB):
                        att_signal(nc.vector.bn_aggr(mv[:, j, :], stats[:, j, :]))
                    att_wait(g)
                    nc.vector.tensor_scalar_add(var_eps[:, tiles], mv[:, tiles, 1], LN_EPS).then_inc(var2, 1)
                assert att_count[0] == ATT_STEPS, att_count

            def normalise_x2(g):
                normalise(g, x2, 0, mv, rstd, rstd2, BG, xn, xn2)

            def split_h2(g):
                for b, cols in enumerate(SEQUENCES):
                    dve.wait_ge(h2_act, BG * g + b + 1)
                    nc.vector.tensor_copy(h2_hi[:, cols], h2[:, cols]).then_inc(h2_split, 1)
                    dve.wait_ge(h2_split, 2 * (BG * g + b) + 1)
                    nc.vector.tensor_tensor(h2_lo[:, cols], h2[:, cols], h2_hi[:, cols].bitcast(F32),
                                            ALU.subtract).then_inc(h2_split, 1)

            def route(g):
                route_count[0] = 0
                dve.wait_ge(logits_mm, g + 1)
                route_signal(nc.vector.tensor_tensor(logits[:], bank_c[:, 0:J * E].rearrange("p (j e) -> p j e", j=J),
                                                     bgate.unsqueeze(1).to_broadcast([P, J, E]), ALU.add))
                route_wait(g)
                one = logits[:].unsqueeze(3).to_broadcast([P, J, E, E])
                other = logits[:].unsqueeze(2).to_broadcast([P, J, E, E])
                route_signal(nc.vector.tensor_tensor(equal[:], other, one, ALU.is_equal))
                for j in range(J):
                    route_signal(nc.vector.max(top[:, j, :], logits[:, j, :]))
                route_wait(g)
                nc.vector.tensor_tensor(gap[:], top[:, :, 1], top[:, :, 0], ALU.subtract).then_inc(gap_done, 1)
                route_signal(nc.vector.tensor_tensor(
                    equal[:], equal[:], before[:].unsqueeze(1).to_broadcast([P, J, E, E]), ALU.mult))
                route_signal(nc.vector.tensor_tensor(larger[:], other, one, ALU.is_gt))
                route_wait(g)
                route_signal(nc.vector.tensor_tensor(larger[:], larger[:], equal[:], ALU.add))
                route_wait(g)
                dve.wait_ge(gap_exp, g + 1)
                nc.vector.tensor_reduce(rank[:], larger[:], AX.X, ALU.add).then_inc(rank_done, 1)
                route_signal(nc.vector.tensor_scalar_add(p_sum[:], p_gap[:], 1.0))
                route_wait(g)
                route_signal(nc.vector.reciprocal(share1[:], p_sum[:]))
                route_wait(g)
                route_signal(nc.vector.tensor_tensor(share2[:], p_gap[:], share1[:], ALU.mult))
                dve.wait_ge(rank_done, g + 1)
                nc.vector.scalar_tensor_tensor(
                    out=comb1[:], in0=rank[:], scalar=0.0, in1=share1[:].unsqueeze(2).to_broadcast([P, J, E]),
                    op0=ALU.is_equal, op1=ALU.mult).then_inc(comb1_done, 1)
                route_wait(g)
                route_signal(nc.vector.scalar_tensor_tensor(
                    out=comb2[:], in0=rank[:], scalar=1.0, in1=share2[:].unsqueeze(2).to_broadcast([P, J, E]),
                    op0=ALU.is_equal, op1=ALU.mult))
                route_wait(g)
                dve.wait_ge(comb1_done, g + 1)
                nc.vector.tensor_tensor(comb[:], comb1[:], comb2[:], ALU.add).then_inc(comb_done, 1)
                assert route_count[0] == ROUTE_STEPS, route_count

            def split_comb(g):
                nc.vector.tensor_copy(comb_hi[:], comb[:]).then_inc(halved, 1)
                dve.wait_ge(halved, 3 * g + 1)
                hi, whole = (c.unsqueeze(1).to_broadcast([P, 2, J, E]) for c in (comb_hi[:].bitcast(F32), comb[:]))
                nc.vector.tensor_copy(comb_halves[:, :, :, 0, :], hi).then_inc(halved, 1)
                nc.vector.tensor_tensor(comb_halves[:, :, :, 1, :], whole, hi, ALU.subtract).then_inc(halved, 1)

            def copy_combT(g):
                dve.wait_ge(comb_T, g + 1)
                nc.vector.tensor_copy(combT[:], bank_c[:, 0:P]).then_inc(combT_done, 1)

            def add_expert(g, e):
                dve.wait_ge(y_mm, E * g + e + 1)
                y = y_ps[e % 2][:].rearrange("p (j d) -> p j d", j=J)
                if e == 0:
                    dve.wait_ge(comb_done, g + 1)
                    dve.wait_ge(acc_free, g + 1)
                if e == B2_AFTER + 1:
                    dve.wait_ge(acc_step, ACC_STEPS * g + acc_steps(B2_AFTER) + 1)
                for j in range(J):
                    weight = comb[:, j, e:e + 1]
                    if e == 0:
                        nc.vector.tensor_scalar(acc[:, j, :], y[:, j, :], weight, None, ALU.mult).then_inc(acc_step, 1)
                        continue
                    if e != B2_AFTER + 1:
                        dve.wait_ge(acc_step, ACC_STEPS * g + acc_steps(e - 1) - J + j + 1)
                    nc.vector.scalar_tensor_tensor(out=acc[:, j, :], in0=y[:, j, :], scalar=weight,
                                                   in1=acc[:, j, :], op0=ALU.mult,
                                                   op1=ALU.add).then_inc(acc_step, 1)

            def add_b2(g):
                dve.wait_ge(b2_mm, g + 1)
                dve.wait_ge(acc_step, ACC_STEPS * g + acc_steps(B2_AFTER))
                nc.vector.tensor_tensor(acc[:].rearrange("p j d -> p (j d)"), bank_c[:],
                                        acc[:].rearrange("p j d -> p (j d)"), ALU.add).then_inc(acc_step, 1)

            def finish_last():
                g, e = G - 1, E - 1
                dve.wait_ge(x2_kept, G)
                dve.wait_ge(acc_free, G)
                dve.wait_ge(result, G - 1)
                for b in range(BG):
                    rows = slice(b * JB, (b + 1) * JB)
                    both = slice(g * J + b * JB, g * J + (b + 1) * JB)
                    dve.wait_ge(y_last, b + 1)
                    for j in range(b * JB, (b + 1) * JB):
                        dve.wait_ge(acc_step, ACC_STEPS * g + acc_steps(e - 1) - J + j + 1)
                        nc.vector.scalar_tensor_tensor(out=acc[:, j, :], in0=LAST_Y[b][:, j * D:(j + 1) * D],
                                                       scalar=comb[:, j, e:e + 1], in1=acc[:, j, :], op0=ALU.mult,
                                                       op1=ALU.add).then_inc(acc_step, 1)
                    dve.wait_ge(acc_step, ACC_STEPS * g + acc_steps(e) - J + (b + 1) * JB)
                    nc.vector.tensor_tensor(scaled[:, rows, :], acc[:, rows, :],
                                            gates[:, g * BG + b, 1, :].unsqueeze(1).to_broadcast([P, JB, D]),
                                            ALU.mult).then_inc(last_step, 1)
                    dve.wait_ge(last_step, b + 1)
                    nc.vector.tensor_tensor(x_all[:, both, :], scaled[:, rows, :], x_all[:, both, :],
                                            ALU.add).then_inc(last_rows, 1)

            def experts(g, following, preparing):
                if following:
                    take_mod(g + 1)
                route(g)
                if following:
                    split_h1(g + 1)
                add_expert(g, 0)
                if following:
                    clamp_a(g + 1, halves_of(bank_b))
                add_expert(g, 1)
                if following:
                    v_of(g + 1)
                if preparing:
                    measure_in(g + 2)
                if following:
                    for b in range(BG):
                        sum_logs(g + 1, b)
                if preparing:
                    normalise_in(g + 2)
                if following:
                    decay_k(g + 1)
                add_expert(g, 2)
                dve.wait_ge(comb_done, g + 1)
                split_comb(g)
                if following:
                    mask_scores(g + 1)
                add_expert(g, 3)
                if following:
                    add_attention(g + 1)
                add_expert(g, 4)
                if following:
                    normalise_x2(g + 1)
                copy_combT(g)
                add_expert(g, 5)
                add_b2(g)
                if following:
                    split_h2(g + 1)
                add_expert(g, 6)
                if following:
                    add_expert(g, 7)
                else:
                    finish_last()

            def take_modulation(i):
                dve.wait_ge(mod_mm, i + 1)
                mod_ps = z_ps[0][:, 2 * i * B:2 * (i + 1) * B].rearrange("p (m b) -> p m b", m=2)
                nc.vector.tensor_copy(mod[:, 2 * i, :], mod_ps[:, 0, :]).then_inc(mod_ready, 1)
                nc.vector.tensor_scalar_add(mod[:, 2 * i + 1, :], mod_ps[:, 1, :], 1.0).then_inc(mod_ready, 1)
                dve.wait_ge(mod_ready, 2 * (i + 1))

            dve.wait_ge(in_x0, 16)
            measure_in(0)
            dve.wait_ge(c_exp_done, 1)
            after_once(nc.vector.tensor_scalar_add(c_den[:], c_exp[:], 1.0))
            after_once(nc.vector.reciprocal(c_rec[:], c_den[:]))
            nc.vector.tensor_tensor(c_silu[:], c_in, c_rec[:], ALU.mult).then_inc(silu_done, 1)
            normalise_in(0)
            take_modulation(0)
            nc.vector.tensor_copy(mod_now[:, 0:2, :], mod[:, 0:2, 0:BG]).then_inc(mod_taken, 1)
            dve.wait_ge(in_watt, 16)
            after_once(nc.vector.tensor_copy(watt_hi[:], watt[:, 0:3, :]))
            nc.vector.tensor_tensor(watt_lo[:], watt[:, 0:3, :], watt_hi[:].bitcast(F32),
                                    ALU.subtract).then_inc(watt_split, 1)
            split_h1(0)
            dve.wait_ge(in_x1, 16)
            stats_of_in(1, (0,))
            dve.wait_ge(g_taken, 2)
            nc.vector.tensor_scalar(g_sign[:], g_raw[:], 0.0, 2.0, ALU.is_ge, ALU.mult).then_inc(gate_step, 1)
            nc.vector.tensor_scalar_max(g_mag[:], g_abs[:], G_LEAST).then_inc(gate_step, 1)
            dve.wait_ge(gate_step, 2)
            nc.vector.scalar_tensor_tensor(out=g_out[:], in0=g_sign[:], scalar=-1.0, in1=g_mag[:],
                                           op0=ALU.add, op1=ALU.mult).then_inc(g_ready, 1)
            clamp_a(0, FIRST_A, True)
            take_modulation(1)
            nc.vector.tensor_copy(mod_now[:, 2:4, :], mod[:, 2:4, 0:BG]).then_inc(mod_late, 1)
            dve.wait_ge(k_mm, 1)
            nc.vector.tensor_scalar(kT[:], bank_c[:], bqka[:, 1:2], 0.0, ALU.add, ALU.max).then_inc(k_done, 1)
            stats_of_in(1, (1,))
            for b, cols in enumerate(SEQUENCES):
                sum_logs(0, b)
                dve.wait_ge(q_mm, 1)
                nc.vector.tensor_scalar(qT[:, cols], bank_d[:, cols], bqka[:, 0:1], 0.0, ALU.add,
                                        ALU.max).then_inc(q_done, 1)
            decay_k(0)
            dve.wait_ge(in_rows, 16)
            dve.wait_ge(v_ones, 1)
            v_of(0)
            dve.wait_ge(pool_const, 5)
            stats_of_in(1, (2,))
            mask_scores(0)
            stats_of_in(1, (3,))
            close_measure_in(1)
            add_attention(0)
            normalise_x2(0)
            split_h2(0)
            normalise_in(1)
            dve.wait_ge(in_rest, 16)
            with dve.Fori(0, G - 2) as g:
                experts(g, True, True)
            experts(G - 2, True, False)
            experts(G - 1, False, False)

        @block.tensor
        def _(pe):
            def mm(dst, lhsT, rhs, start=True, stop=True):
                return nc.tensor.matmul(dst, lhsT, rhs, start=start, stop=stop)

            def in_halves(dst, w_hi, w_lo, m_hi, m_lo):
                mm(dst, w_hi, m_hi, stop=False)
                mm(dst, w_hi, m_lo, start=False, stop=False)
                return mm(dst, w_lo, m_hi, start=False)

            def transpose_rows(g, rows, ready, places, done):
                for b in range(BG):
                    pe.wait_ge(ready, J * g + (b + 1) * JB)
                    for j in range(JB):
                        last = nc.tensor.transpose(places[b][:, j * P:(j + 1) * P], rows[:, b * JB + j, :], ident[:])
                    last.then_inc(done, 1)

            def a_and_k(g, places):
                for b, cols in enumerate(SEQUENCES):
                    pe.wait_ge(h1_split, BG * g + b + 1)
                    in_halves(places[b], watt_hi[:, 2, :], watt_lo[:, 2, :],
                              h1_hi[:, cols], h1_lo[:, cols]).then_inc(a_mm, 1)
                in_halves(bank_c[:], watt_hi[:, 1, :], watt_lo[:, 1, :], h1_hi[:], h1_lo[:]).then_inc(k_mm, 1)

            def v_of(g):
                for j in range(J):
                    last = mm(bank_a[:, j * D:(j + 1) * D], h1[:, j * P:(j + 1) * P], watt[:, 3, :])
                last.then_inc(v_mm, 1)

            def q_of(g):
                in_halves(bank_d[:], watt_hi[:, 0, :], watt_lo[:, 0, :], h1_hi[:], h1_lo[:]).then_inc(q_mm, 1)

            def scores_of(g):
                for b, ps in enumerate((bank_b, bank_c)):
                    t0 = b * S
                    pe.wait_ge(q_done, BG * g + b + 1)
                    pe.wait_ge(wk_done, BG * g + b + 1)
                    mm(ps[:, 0:S], wkT[:, t0:t0 + P], qT[:, t0:t0 + S])
                    mm(ps[:, S:SC], wkT[:, t0 + P:t0 + S], qT[:, t0 + P:t0 + S]).then_inc(s_mm, 1)

            def values_of(g):
                for b, ps in enumerate((bank_d, bank_a)):
                    pe.wait_ge(v_gated, BG * g + b + 1)
                    pe.wait_ge(s_masked, BG * g + b + 1)
                    mm(ps[:, 0:D + 1], scores[:, b, 0:P], v[:, b * JB, 0:D + 1])
                    mm(ps[:, S:S + D + 1], scores[:, b, P:S], v[:, b * JB, 0:D + 1], stop=False)
                    mm(ps[:, S:S + D + 1], scores[:, b, S:SC], v[:, b * JB + 1, 0:D + 1],
                       start=False).then_inc(av_mm, 1)

            def logits_of(g):
                if not isinstance(g, int) or g > 0:
                    pe.wait_ge(acc_step, ACC_STEPS * (g - 1) + acc_steps(B2_AFTER) + 1)
                for j in range(J):
                    if j % JB == 0:
                        pe.wait_ge(h2_act, BG * g + j // JB + 1)
                    last = mm(bank_c[:, j * E:(j + 1) * E], h2[:, j * P:(j + 1) * P], wg)
                last.then_inc(logits_mm, 1)

            def transpose_comb(g):
                pe.wait_ge(halved, 3 * (g + 1))
                nc.tensor.transpose(bank_c[:, 0:P], comb_halves[:].rearrange("p r j h e -> p (r j h e)"),
                                    ident[:]).then_inc(comb_T, 1)

            def b2_of(g):
                pe.wait_ge(combT_done, g + 1)
                pe.wait_ge(b2_split, 1)
                mm(bank_c[:], combT[:], b2_halves[:].rearrange("k j d -> k (j d)")).then_inc(b2_mm, 1)

            def hidden(g, e):
                if e % 2 == 0:
                    pe.wait_ge(w1_split, e // 2 + 1)
                for hb in range(HB):
                    if e > 0:
                        pe.wait_ge(relu_done, HB * (E * g + e - 1) + hb + 1)
                    w = slice((HB * e + hb) * P, (HB * e + hb + 1) * P)
                    in_halves(z_ps[hb][:], w1_hi[:, w], w1_lo[:, w], h2_hi[:], h2_lo[:]).then_inc(z_mm, 1)

            def expert_out(g, e):
                pe.wait_ge(relu_done, HB * (E * g + e) + HB)
                if e >= 2:
                    pe.wait_ge(acc_step, ACC_STEPS * g + acc_steps(e - 2))
                else:
                    pe.wait_ge(gap_done, g + 1)
                last_one = isinstance(g, int) and e == E - 1
                for j in range(J):
                    out_ps = LAST_Y[j // JB] if last_one else y_ps[e % 2]
                    for hb in range(HB):
                        last = mm(out_ps[:, j * D:(j + 1) * D], relu[:, e % 2, hb, j * P:(j + 1) * P],
                                  w2[:, e, hb, :], start=hb == 0, stop=hb == HB - 1)
                    if last_one and j % JB == JB - 1:
                        last.then_inc(y_last, 1)
                if not last_one:
                    last.then_inc(y_mm, 1)

            def experts(g, following):
                hidden(g, 0)
                if following:
                    transpose_rows(g + 1, xn_in, xn1, halves_of(bank_a), xn1_T)
                hidden(g, 1)
                expert_out(g, 0)
                hidden(g, 2)
                if following:
                    a_and_k(g + 1, halves_of(bank_b))
                expert_out(g, 1)
                hidden(g, 3)
                if following:
                    v_of(g + 1)
                    q_of(g + 1)
                expert_out(g, 2)
                hidden(g, 4)
                expert_out(g, 3)
                if following:
                    scores_of(g + 1)
                hidden(g, 5)
                if following:
                    values_of(g + 1)
                expert_out(g, 4)
                hidden(g, 6)
                transpose_comb(g)
                expert_out(g, 5)
                hidden(g, 7)
                b2_of(g)
                if following:
                    transpose_rows(g + 1, xn, xn2, halves_of(bank_b), xn2_T)
                expert_out(g, 6)
                expert_out(g, 7)
                if following:
                    logits_of(g + 1)
                    pe.wait_ge(h2_split, 2 * BG * (g + 2))

            def keep_warm(count):
                for _ in range(count):
                    nc.tensor.transpose(z_ps[1][:, 0:P], ident[:], ident[:])

            pe.wait_ge(ident_made, 1)
            keep_warm(WARM_START)
            def modulation(places, chunks):
                for place, chunk in zip(places, chunks):
                    last = mm(z_ps[0][:, place * B:(place + 1) * B], wm[:, chunk, :], c_silu[:])
                last.then_inc(mod_mm, 1)

            pe.wait_ge(in_wmod_a, 16)
            pe.wait_ge(silu_done, 1)
            modulation((0, 1), (0, 1))
            transpose_rows(0, xn_in, xn1, FIRST_XN1, xn1_T)
            pe.wait_ge(in_wmod_b, 16)
            for i, chunk in enumerate((2, 5)):
                last = mm(y_ps[0][0:B, i * D:(i + 1) * D], c_silu[:], wm[:, chunk, :])
            last.then_inc(gate_mm, 1)
            pe.wait_ge(mod_ready, 2)
            modulation((2, 3), (3, 4))
            keep_warm(WARM_SPLIT)
            pe.wait_ge(watt_split, 1)
            a_and_k(0, FIRST_A)
            q_of(0)
            v_of(0)
            keep_warm(WARM_DECAY)
            scores_of(0)
            keep_warm(WARM_MASK)
            values_of(0)
            keep_warm(WARM_NORM)
            transpose_rows(0, xn, xn2, FIRST_XN2, xn2_T)
            keep_warm(WARM_H2)
            pe.wait_ge(in_columns, 16)
            logits_of(0)
            pe.wait_ge(h2_split, 2 * BG)
            pe.wait_ge(in_w2, 16)
            with pe.Fori(0, G - 1) as g:
                experts(g, True)
            experts(G - 1, False)


def kernel(**inputs):
    import numpy as np
    import concourse.bacc as bacc
    from concourse.bass_utils import run_bass_kernel_spmd

    def a(name):
        return np.asarray(inputs["L0_" + name])

    arrays = {
        "x": a("attn_x_seq").reshape(T, D),
        "w_att": np.concatenate([a(f"attn_W_{m}").T for m in "qkav"], axis=1),
        "column_inputs": np.concatenate([a("c").T, np.stack([a(f"attn_b_{m}") for m in "qka"], axis=1),
                                   a("ffn_b1").reshape(E * HB, P).T, a("ffn_Wg").T], axis=1),
        "row_inputs": np.concatenate([a("attn_b_v"), a("ffn_bg")]),
        "w1t": a("ffn_W1").transpose(2, 0, 1).reshape(D, E * H),
        "w2t": a("ffn_W2").reshape(E, D, HB, P).transpose(3, 0, 2, 1).reshape(P, E * HB * D),
        "b2": np.concatenate([a("ffn_b2")] * 2),
        "wmod": a("wmod"),
    }
    arrays = {name: np.ascontiguousarray(value) for name, value in arrays.items()}
    nc = bacc.Bacc("TRN2", target_bir_lowering=False, num_devices=1)
    args = {name: nc.dram_tensor(f"{name}_dram", value.shape, F32, kind="ExternalInput").ap()
            for name, value in arrays.items()}
    out = nc.dram_tensor("out_dram", (T, D), F32, kind="ExternalOutput").ap()
    gate_rows = nc.dram_tensor("gate_rows", (B, 2 * D), F32, kind="Internal").ap()
    adaln_block(nc, out=out, gate_rows=gate_rows, **args)
    got = run_bass_kernel_spmd(nc, [{f"{name}_dram": value for name, value in arrays.items()}], core_ids=[0])
    return got.results[0]["out_dram"].reshape(B, S, D)
```
